# Optimizing a Trainium2 kernel written in Bass

```python
import numpy as np
import jax
import jax.numpy as jnp

def _softmax(x, axis=-1):
    return jax.nn.softmax(x, axis=axis)

def _gelu(x):
    return jax.nn.gelu(x, approximate=True)

def _silu(x):
    return jax.nn.silu(x)

def _sigmoid(x):
    return jax.nn.sigmoid(x)

def _layernorm(x, axis=-1, eps=1e-05):
    m = jnp.mean(x, axis=axis, keepdims=True)
    v = jnp.var(x, axis=axis, keepdims=True)
    return (x - m) / jnp.sqrt(v + eps)

def _scatter_add(tgt, idx, src, axis=0):
    return tgt.at[idx].add(src)

def _segment_sum(src, seg, n):
    return jax.ops.segment_sum(src, seg, n)
kernel_name = 'mk_gnn_preln_d2_gnn_r8_2c064e'

def setup_inputs(seed: int=0):
    np.random.seed(seed)
    _w = jnp.asarray

    def _rec_inputs():
        import jax
        import jax.numpy as jnp
        _gk = jax.random.key(seed)
        x = -8.776e-05 + 1 * jax.random.normal(jax.random.fold_in(_gk, 1), (1250, 512), jnp.float32)
        src = jax.random.randint(jax.random.fold_in(_gk, 2), (20000,), 0, 1250, jnp.int32)
        dst = jnp.minimum((1250 * jax.random.uniform(jax.random.fold_in(_gk, 3), (20000,)) ** 2.0).astype(jnp.int32), 9999)
        _o = jnp.argsort(dst, stable=True)
        src = src[_o]
        dst = dst[_o]
        return (x, src, dst)
    x, src, dst = _rec_inputs()

    def _L0_gnn_setup():
        import jax, jax.numpy as jnp
        import numpy as np
        N_EMBD = 512
        HEADS = 8
        C = N_EMBD // HEADS
        N_NODES = 1250
        N_EDGES = 20000
        NEG_SLOPE = 0.2
        LN_EPS = 1e-05

        def _layer_norm(x, g, b):
            mu = jnp.mean(x, axis=-1, keepdims=True)
            var = jnp.mean(jnp.square(x - mu), axis=-1, keepdims=True)
            return (x - mu) * jax.lax.rsqrt(var + LN_EPS) * g + b

        def _gatv2(x, edge_index, Wl, Wr, att, gat_bias):
            src, dst = (edge_index[0], edge_index[1])
            xl = (x @ Wl).reshape(-1, HEADS, C)
            xr = (x @ Wr).reshape(-1, HEADS, C)
            h = jax.nn.leaky_relu(xl[src] + xr[dst], NEG_SLOPE)
            e = jnp.einsum('ehc,hc->eh', h, att)
            m = jax.ops.segment_max(e, dst, num_segments=N_NODES)
            ex = jnp.exp(e - m[dst])
            denom = jax.ops.segment_sum(ex, dst, num_segments=N_NODES)
            alpha = ex / (denom[dst] + 1e-16)
            msg = alpha[..., None] * xl[src]
            out = jax.ops.segment_sum(msg, dst, num_segments=N_NODES)
            return out.reshape(-1, HEADS * C) + gat_bias
        key = jax.random.key(seed)
        ks = jax.random.split(key, 12)
        s = 0.02
        x = jax.random.normal(ks[0], (N_NODES, N_EMBD), dtype=jnp.float32)
        edge_index = jax.random.randint(ks[1], (2, N_EDGES), 0, N_NODES, dtype=jnp.int32)
        return {'x': x, 'edge_index': edge_index, 'ln1_g': jnp.ones((N_EMBD,), jnp.float32), 'ln1_b': jnp.zeros((N_EMBD,), jnp.float32), 'Wl': jax.random.normal(ks[2], (N_EMBD, HEADS * C), jnp.float32) * s, 'Wr': jax.random.normal(ks[3], (N_EMBD, HEADS * C), jnp.float32) * s, 'att': jax.random.normal(ks[4], (HEADS, C), jnp.float32) * s, 'gat_bias': jnp.zeros((HEADS * C,), jnp.float32), 'ln2_g': jnp.ones((N_EMBD,), jnp.float32), 'ln2_b': jnp.zeros((N_EMBD,), jnp.float32), 'W1': jax.random.normal(ks[5], (N_EMBD, 4 * N_EMBD), jnp.float32) * s, 'b1': jnp.zeros((4 * N_EMBD,), jnp.float32), 'W2': jax.random.normal(ks[6], (4 * N_EMBD, N_EMBD), jnp.float32) * s, 'b2': jnp.zeros((N_EMBD,), jnp.float32)}
    _L0_gnn_all = _L0_gnn_setup()
    _L0_gnn_in = {k: v for k, v in _L0_gnn_all.items() if k in ('ln1_g', 'ln1_b', 'Wl', 'Wr', 'att', 'gat_bias', 'ln2_g', 'ln2_b', 'W1', 'b1', 'W2', 'b2')}
    del _L0_gnn_all

    def _L1_gnn_setup():
        import jax, jax.numpy as jnp
        import numpy as np
        N_NODES = 2500
        N_EDGES = 40000
        D = 512
        N_LAYERS = 3
        LN_EPS = 1e-05
        key = jax.random.key(seed)
        k0, k1, k2, k3 = jax.random.split(key, 4)
        feats = jax.random.normal(k0, (N_NODES, D), dtype=jnp.float32)
        src = jax.random.randint(k1, (N_EDGES,), 0, N_NODES)
        dst = jax.random.randint(k2, (N_EDGES,), 0, N_NODES)
        ln_g = jnp.ones((N_LAYERS, D), dtype=jnp.float32)
        ln_b = jnp.zeros((N_LAYERS, D), dtype=jnp.float32)
        W = jax.random.normal(k3, (N_LAYERS, D, D), dtype=jnp.float32) * (1.0 / np.sqrt(D)).astype(np.float32)
        b = jnp.zeros((N_LAYERS, D), dtype=jnp.float32)
        return {'feats': feats, 'src': src, 'dst': dst, 'ln_g': ln_g, 'ln_b': ln_b, 'W': W, 'b': b}
    _L1_gnn_all = _L1_gnn_setup()
    _L1_gnn_in = {k: v for k, v in _L1_gnn_all.items() if k in ('ln_g', 'ln_b', 'W', 'b')}
    del _L1_gnn_all
    return {'x': x, 'src': src, 'dst': dst, 'L0_gnn_ln1_g': _L0_gnn_in['ln1_g'], 'L0_gnn_ln1_b': _L0_gnn_in['ln1_b'], 'L0_gnn_Wl': _L0_gnn_in['Wl'], 'L0_gnn_Wr': _L0_gnn_in['Wr'], 'L0_gnn_att': _L0_gnn_in['att'], 'L0_gnn_gat_bias': _L0_gnn_in['gat_bias'], 'L0_gnn_ln2_g': _L0_gnn_in['ln2_g'], 'L0_gnn_ln2_b': _L0_gnn_in['ln2_b'], 'L0_gnn_W1': _L0_gnn_in['W1'], 'L0_gnn_b1': _L0_gnn_in['b1'], 'L0_gnn_W2': _L0_gnn_in['W2'], 'L0_gnn_b2': _L0_gnn_in['b2'], 'L1_gnn_ln_g': _L1_gnn_in['ln_g'], 'L1_gnn_ln_b': _L1_gnn_in['ln_b'], 'L1_gnn_W': _L1_gnn_in['W'], 'L1_gnn_b': _L1_gnn_in['b']}

def reference(x, src, dst, L0_gnn_ln1_g, L0_gnn_ln1_b, L0_gnn_Wl, L0_gnn_Wr, L0_gnn_att, L0_gnn_gat_bias, L0_gnn_ln2_g, L0_gnn_ln2_b, L0_gnn_W1, L0_gnn_b1, L0_gnn_W2, L0_gnn_b2, L1_gnn_ln_g, L1_gnn_ln_b, L1_gnn_W, L1_gnn_b):
    import jax
    import jax.numpy as jnp

    def _L0_gnn_ref(x, edge_index, ln1_g, ln1_b, Wl, Wr, att, gat_bias, ln2_g, ln2_b, W1, b1, W2, b2):
        import jax, jax.numpy as jnp
        import numpy as np
        N_EMBD = 512
        HEADS = 8
        C = N_EMBD // HEADS
        N_NODES = 1250
        N_EDGES = 20000
        NEG_SLOPE = 0.2
        LN_EPS = 1e-05

        def _layer_norm(x, g, b):
            mu = jnp.mean(x, axis=-1, keepdims=True)
            var = jnp.mean(jnp.square(x - mu), axis=-1, keepdims=True)
            return (x - mu) * jax.lax.rsqrt(var + LN_EPS) * g + b

        def _gatv2(x, edge_index, Wl, Wr, att, gat_bias):
            src, dst = (edge_index[0], edge_index[1])
            xl = (x @ Wl).reshape(-1, HEADS, C)
            xr = (x @ Wr).reshape(-1, HEADS, C)
            h = jax.nn.leaky_relu(xl[src] + xr[dst], NEG_SLOPE)
            e = jnp.einsum('ehc,hc->eh', h, att)
            m = jax.ops.segment_max(e, dst, num_segments=N_NODES)
            ex = jnp.exp(e - m[dst])
            denom = jax.ops.segment_sum(ex, dst, num_segments=N_NODES)
            alpha = ex / (denom[dst] + 1e-16)
            msg = alpha[..., None] * xl[src]
            out = jax.ops.segment_sum(msg, dst, num_segments=N_NODES)
            return out.reshape(-1, HEADS * C) + gat_bias
        h = _layer_norm(x, ln1_g, ln1_b)
        h = _gatv2(h, edge_index, Wl, Wr, att, gat_bias)
        x = x + h
        h = _layer_norm(x, ln2_g, ln2_b)
        h = jax.nn.gelu(h @ W1 + b1, approximate=False) @ W2 + b2
        return x + h

    def _L1_gnn_ref(feats, src, dst, ln_g, ln_b, W, b):
        import jax, jax.numpy as jnp
        import numpy as np
        N_NODES = 2500
        N_EDGES = 40000
        D = 512
        N_LAYERS = 3
        LN_EPS = 1e-05
        n = feats.shape[0]
        ones_e = jnp.ones(src.shape[0], dtype=feats.dtype)
        out_deg = jnp.maximum(jax.ops.segment_sum(ones_e, src, num_segments=n), 1.0)
        in_deg = jnp.maximum(jax.ops.segment_sum(ones_e, dst, num_segments=n), 1.0)
        norm_src = jax.lax.rsqrt(out_deg)[:, None]
        norm_dst = jax.lax.rsqrt(in_deg)[:, None]
        h = feats
        L = W.shape[0]
        for i in range(L):
            mu = jnp.mean(h, axis=-1, keepdims=True)
            var = jnp.mean(jnp.square(h - mu), axis=-1, keepdims=True)
            h = (h - mu) * jax.lax.rsqrt(var + LN_EPS) * ln_g[i] + ln_b[i]
            h = h * norm_src @ W[i]
            msg = h[src]
            agg = jax.ops.segment_sum(msg, dst, num_segments=n)
            h = agg * norm_dst + b[i]
            if i < L - 1:
                h = jax.nn.relu(h)
        return h
    edge_index = jnp.stack([src, dst])
    h = jnp.maximum(_layernorm(x, axis=-1), 0.0)
    x = x + _L0_gnn_ref(h, edge_index, L0_gnn_ln1_g, L0_gnn_ln1_b, L0_gnn_Wl, L0_gnn_Wr, L0_gnn_att, L0_gnn_gat_bias, L0_gnn_ln2_g, L0_gnn_ln2_b, L0_gnn_W1, L0_gnn_b1, L0_gnn_W2, L0_gnn_b2)
    h = jnp.maximum(_layernorm(x, axis=-1), 0.0)
    x = x + _L1_gnn_ref(h, src, dst, L1_gnn_ln_g, L1_gnn_ln_b, L1_gnn_W, L1_gnn_b)
    return x

_drawn_inputs = setup_inputs


def setup_inputs(seed=0):
    import zlib

    import numpy as np

    out = dict(_drawn_inputs(seed))
    spreads = {'L0_gnn_ln1_g': (1.0, 0.6),
     'L0_gnn_ln1_b': (0.0, 0.1),
     'L0_gnn_gat_bias': (0.0, 0.1),
     'L0_gnn_ln2_g': (1.0, 0.548),
     'L0_gnn_ln2_b': (0.0, 0.1),
     'L0_gnn_b1': (0.0, 0.1),
     'L0_gnn_b2': (0.0, 0.1),
     'L1_gnn_ln_g': (1.0, 0.2),
     'L1_gnn_ln_b': (0.0, 0.1),
     'L1_gnn_b': (0.0, 0.1)}
    factors = {'L0_gnn_Wr': 8.0, 'L0_gnn_att': 8.0}
    for name, (base, spread) in spreads.items():
        noise = np.random.default_rng([zlib.crc32(name.encode()), seed]).standard_normal(out[name].shape)
        drawn = base * np.exp(spread * noise) if base else spread * noise
        out[name] = jnp.asarray(drawn.astype(out[name].dtype))
    for name, factor in factors.items():
        out[name] = (out[name] * factor).astype(out[name].dtype)
    return out
```

```python
from contextlib import ExitStack

import concourse.bass as bass
from concourse import mybir

ALU = mybir.AluOpType
ACT = mybir.ActivationFunctionType
AX = mybir.AxisListType
F32 = mybir.dt.float32
BF16 = mybir.dt.bfloat16
FP16 = mybir.dt.float16
I32 = mybir.dt.int32

P = 128
ROUND = 1.5 * 2.0 ** 23
FAR = -1.0e30
LN_EPS = 1e-5
SLOPE = 0.2


class Queue:

    def __init__(self, sem):
        self.sem, self.count, self.ops, self.seen = sem, 0, [], {}

    def wait(self, *after):
        for token in after:
            if token is None:
                continue
            sem, value = token
            if self.seen.get(id(sem), 0) < value:
                self.seen[id(sem)] = value
                self.ops.append(lambda e, sem=sem, value=value: e.wait_ge(sem, value))

    def do(self, fn, *after):
        self.wait(*after)
        self.count += 1
        self.ops.append(lambda e: fn(e).then_inc(self.sem, 1))
        return (self.sem, self.count)

    def quiet(self, fn, *after):
        self.wait(*after)
        self.ops.append(fn)

    def run(self, engine):
        for op in self.ops:
            op(engine)


class Landing:

    def __init__(self, sem):
        self.sem, self.count = sem, 0

    def dma(self, queue, fn, *after):
        queue.wait(*after)
        self.count += 16
        queue.ops.append(lambda e: fn(e).then_inc(self.sem, 16))
        return (self.sem, self.count)


def build(nc, ins, out):
    N, D = ins["x"].shape
    E = ins["src"].shape[0]
    HEADS, C = ins["L0_gnn_att"].shape
    F = ins["L0_gnn_W1"].shape[1]
    LAYERS = ins["L1_gnn_W"].shape[0]
    NB = -(-N // P)
    NP = NB * P
    LAST = N - (NB - 1) * P
    KC = D // P
    FC = F // P
    EP = 125
    EJ = E // EP
    LOW = 32
    HIGH = NP // LOW
    HPB = P // LOW
    PACK = 2048
    PAIR = 2 * P
    NG = (E + NB * (PAIR - 1)) // PAIR
    NC = 2 * NG
    TW = D + HEADS
    SG = P // HEADS
    SK = NC // SG
    RUN = SK * P
    GROUP = 3
    assert E == EP * EJ and N < PACK // 1 and SG * SK == NC and NP % LOW == 0

    with ExitStack() as ctx:
        sem = lambda n: ctx.enter_context(nc.semaphore(n))
        V, A, T, G, S = [Queue(sem("s_" + n)) for n in ("vector", "scalar", "tensor", "gpsimd", "sync")]
        landings = []

        def landing(name):
            landings.append(Landing(sem("d_" + name)))
            return landings[-1]

        def sb(name, shape, dt=F32):
            return ctx.enter_context(nc.sbuf_tensor(name, shape, dt))

        left_table = nc.dram_tensor("left_table", (NP, TW), F32, kind="Internal").ap()
        right_table = nc.dram_tensor("right_table", (NP, TW), F32, kind="Internal").ap()

        bank = ctx.enter_context(nc.psum_tensor("bank", [P, 8, 512], F32))
        flat = bank[:, :, :].rearrange("p b n -> p (b n)")

        ident = sb("ident", [P, P])
        ones = sb("ones", [P, P])
        earlier = sb("earlier", [P, P])
        iota = sb("iota", [P, max(NC, EJ)])
        iota_node = sb("iota_node", [P, NP], FP16)
        is_head = sb("is_head", [P, HEADS])
        is_run = sb("is_run", [P, SG])
        to_rows = sb("to_rows", [HEADS, P])
        columns_in = sb("columns_in", [56, P])
        columns = sb("columns", [P, 56])
        att_relu = sb("att_relu", [P, D])
        att_linear = sb("att_linear", [P, D])
        gat_bias = sb("gat_bias", [P, D])
        b2 = sb("b2", [P, D])
        layer_bias = sb("layer_bias", [P, LAYERS, D])
        eps = sb("eps", [P, 1])
        state = sb("state", [P, NB, D])
        counts = sb("counts", [P, NB, NP])
        src_of = sb("src_of", [P, NC], I32)
        dst_of = sb("dst_of", [P, NC], I32)
        src_f = sb("src_f", [P, NC])
        key = sb("key", [P, NC])
        local = sb("local", [P, NC])
        block_of = sb("block_of", [1, NG], I32)
        stat = sb("stat", [P, 2, 6])
        moments = sb("moments", [P, 2, 2])
        deviation = sb("deviation", [P, 2, 1])
        rstd = sb("rstd", [P, 2, 1])
        norm_src = sb("norm_src", [P, NB])
        norm_dst = sb("norm_dst", [P, NB])
        SIZE = 29120
        arena = sb("arena", [P, SIZE])

        class Plan:

            def __init__(self, at, end=SIZE, base=arena):
                self.at, self.end, self.base = at, end, base

            def take(self, *shape, dt=F32, words=None):
                size = 1
                for n in shape:
                    size *= n
                words = size if dt in (F32, I32) else -(-size // 2)
                assert self.at + words <= self.end, (self.at, words, self.end)
                ap = self.base[:, self.at:self.at + words]
                self.at += words
                if dt is not F32:
                    ap = ap.bitcast(dt)
                if len(shape) > 1:
                    names = " ".join(f"a{i}" for i in range(len(shape)))
                    ap = ap.rearrange(f"p ({names}) -> p {names}", **{f"a{i}": n for i, n in enumerate(shape)})
                return ap

        def over(ap, axis, n):
            shape = list(ap.shape)
            shape.insert(axis, n)
            return ap.unsqueeze(axis).broadcast_to(shape)

        plan = Plan(0)
        x_in = plan.take(NB, D)
        trans = plan.take(KC, NP)
        w_left = plan.take(KC, D)
        w_right = plan.take(KC, D)
        wa = plan.take(2, KC, HEADS)
        rows = [plan.take(D) for _ in range(2)]
        tile = [plan.take(TW) for _ in range(4)]
        scratch = plan.take(KC * D)
        sort = Plan(0, NB * NP, counts[:, :, :].rearrange("p b n -> p (b n)"))
        digit = sort.take(EJ, dt=BF16)
        digits = sort.take(HIGH, EJ, dt=BF16)
        match = sort.take(HIGH * EJ, dt=BF16)
        running = sort.take(HIGH * EJ, dt=BF16)
        rest = Plan(plan.at)
        ranked = rest.take(HIGH * EJ)
        src_in, dst_in, digit_i = sort.take(EJ, dt=I32), sort.take(EJ, dt=I32), sort.take(EJ, dt=I32)
        src_g, dst_g, packed, place, place_hi, place_lo = [sort.take(EJ) for _ in range(6)]
        pick_row = [sort.take(P) for _ in range(4)]
        pick_col = [sort.take(max(NC, EJ)) for _ in range(4)]
        total, shifted, per_digit, base_of = [sort.take(HIGH) for _ in range(4)]
        sums = sort.take(HIGH)
        block_end, block_before, block_n, pairs, pair_end, pair_at, shift = [sort.take(NB) for _ in range(7)]
        late = Plan(0, KC * D, scratch)
        passed, block_f = late.take(NG * (NB - 1)), late.take(NG)
        slots_i, part_i = late.take(NC, dt=I32), late.take(NC, dt=I32)

        l_edges, l_x, l_w = landing("edges"), landing("x"), landing("w")
        l_vec, l_wide = landing("vectors"), landing("wide")
        edge_view = lambda ap: ap.rearrange("(p j) -> p j", j=EJ)
        l_edges.dma(S, lambda e: e.dma_start(src_in[0:EP, :], edge_view(ins["src"])))
        edges_in = l_edges.dma(S, lambda e: e.dma_start(dst_in[0:EP, :], edge_view(ins["dst"])))
        PAD_FROM = LAST // 32 * 32
        t_pad = G.do(lambda e: e.memset(x_in[PAD_FROM:P, NB - 1, :], 0.0))
        l_x.dma(S, lambda e: e.dma_start(x_in[:, 0:NB - 1, :], ins["x"][0:(NB - 1) * P, :].rearrange("(b p) d -> p b d", p=P)))
        x_loaded = l_x.dma(S, lambda e: e.dma_start(x_in[0:LAST, NB - 1, :], ins["x"][(NB - 1) * P:N, :]), t_pad)
        vectors = {}
        at = 0
        for name, n in (("L0_gnn_ln1_g", KC), ("L0_gnn_ln1_b", KC), ("L0_gnn_ln2_g", KC), ("L0_gnn_ln2_b", KC),
                        ("L1_gnn_ln_g", KC * LAYERS), ("L1_gnn_ln_b", KC * LAYERS), ("L0_gnn_b1", FC)):
            src = ins[name] if len(ins[name].shape) == 1 else ins[name].rearrange("l d -> (l d)")
            vectors_in = l_vec.dma(S, lambda e, at=at, n=n, src=src: e.dma_start(columns_in[at:at + n, :], src.rearrange("(k p) -> k p", p=P)))
            vectors[name] = at
            at += n
        assert at == 56
        column = lambda name, k: columns[:, vectors[name] + k:vectors[name] + k + 1]
        spread = lambda ap: ap.unsqueeze(0).broadcast_to([P, ap.shape[0]])
        w_view = lambda ap: ap.rearrange("(k p) n -> p k n", p=P)
        l_wide.dma(S, lambda e: e.dma_start(att_relu[:, :], spread(ins["L0_gnn_att"].rearrange("h c -> (h c)"))))
        l_w.dma(S, lambda e: e.dma_start(w_left, w_view(ins["L0_gnn_Wl"])))
        w_loaded = l_w.dma(S, lambda e: e.dma_start(w_right, w_view(ins["L0_gnn_Wr"])))
        l_wide.dma(S, lambda e: e.dma_start(gat_bias[:, :], spread(ins["L0_gnn_gat_bias"])))
        l_wide.dma(S, lambda e: e.dma_start(b2[:, :], spread(ins["L0_gnn_b2"])))
        for i in range(LAYERS):
            wide_in = l_wide.dma(S, lambda e, i=i: e.dma_start(layer_bias[:, i, :], spread(ins["L1_gnn_b"][i, :])))

        g0 = G.do(lambda e: e.iota(digits, [[1, HIGH], [0, EJ]], base=0, channel_multiplier=0, allow_small_or_imprecise_dtypes=True), t_pad)
        t_digits = g0
        G.do(lambda e: e.memset(ident[:, :], 0.0))
        g1 = G.do(lambda e: e.memset(ones[:, :], 1.0))
        g2 = G.do(lambda e: e.affine_select(out=ident[:, :], in_=ident[:, :], compare_op=ALU.not_equal, fill=1.0,
                                            base=0, pattern=[[-1, P]], channel_multiplier=1), g1)
        g3 = G.do(lambda e: e.affine_select(out=earlier[:, :], in_=ones[:, :], compare_op=ALU.is_ge, fill=0.0,
                                            base=-1, pattern=[[1, P]], channel_multiplier=-1), g1)
        G.do(lambda e: e.iota(iota[:, :], [[1, max(NC, EJ)]], base=0, channel_multiplier=0, allow_small_or_imprecise_dtypes=True))
        G.do(lambda e: e.memset(eps[:, :], LN_EPS))
        t_const = G.do(lambda e: e.iota(iota_node[:, :], [[1, NP]], base=0, channel_multiplier=0, allow_small_or_imprecise_dtypes=True))

        V.do(lambda e: e.tensor_reduce(is_head[:, :], ident[:, :].rearrange("p (g h) -> p h g", h=HEADS), AX.X, ALU.add), t_const)
        V.do(lambda e: e.tensor_reduce(is_run[:, :], ident[:, :].rearrange("p (g h) -> p g h", h=HEADS), AX.X, ALU.add))
        V.do(lambda e: e.tensor_copy(to_rows[:, :].rearrange("q (g h) -> q g h", h=HEADS), over(ident[0:HEADS, 0:HEADS], 1, SG)))

        t = T.do(lambda e: e.transpose(bank[:, 7, 0:56], columns_in[:, :], ident[0:56, 0:56]), t_const, vectors_in)
        columns_ready = A.do(lambda e: e.activation(columns[:, :], bank[:, 7, 0:56], ACT.Copy), t)

        R0 = slice(0, EP)

        def ranks(radix, after, shift_for=None):
            m3 = match[R0, 0:radix * EJ].rearrange("p (k j) -> p k j", j=EJ)
            s3 = running[R0, 0:radix * EJ].rearrange("p (k j) -> p k j", j=EJ)
            r3 = ranked[R0, 0:radix * EJ].rearrange("p (k j) -> p k j", j=EJ)
            t = V.do(lambda e: e.tensor_tensor(m3, over(digit[R0, :], 1, radix), digits[R0, 0:radix, :], ALU.is_equal), t_digits, after)
            t = V.do(lambda e: e.tensor_tensor_scan(running[R0, 0:radix * EJ], match[R0, 0:radix * EJ], match[R0, 0:radix * EJ], 0.0, ALU.add, ALU.max), t)
            t1 = V.do(lambda e: e.memset(shifted[R0, 0:1], 0.0))
            t2 = V.do(lambda e: e.tensor_copy(total[R0, 0:radix], s3[:, :, EJ - 1]), t)
            t3 = V.do(lambda e: e.tensor_copy(shifted[R0, 1:radix], s3[:, 0:radix - 1, EJ - 1]))
            t4 = V.do(lambda e: e.tensor_tensor(per_digit[R0, 0:radix], total[R0, 0:radix], shifted[R0, 0:radix], ALU.subtract), t1, t2, t3)
            T.quiet(lambda e: e.matmul(bank[R0, 6, 0:radix], ones[R0, R0], shifted[R0, 0:radix], start=True, stop=False), t_const, t4)
            t5 = T.do(lambda e: e.matmul(bank[R0, 6, 0:radix], earlier[R0, R0], per_digit[R0, 0:radix], start=False, stop=True))
            t6 = V.do(lambda e: e.scalar_tensor_tensor(base_of[R0, 0:radix], bank[R0, 6, 0:radix], -1.0, shifted[R0, 0:radix], ALU.add, ALU.subtract), t5)
            if shift_for is not None:
                t6 = shift_for(t6)
            t7 = V.do(lambda e: e.tensor_tensor(r3, s3, over(base_of[R0, 0:radix], 2, EJ), ALU.add), t6)
            t8 = V.do(lambda e: e.tensor_tensor(r3, r3, m3, ALU.mult), t7)
            return V.do(lambda e: e.tensor_reduce(place[R0, :], r3.rearrange("p k j -> p j k"), AX.X, ALU.add), t8)

        def divide(quotient, value, by, after, remainder=None):
            t = V.do(lambda e: e.tensor_scalar(quotient, value, 1.0 / by, -(by - 1) / 2.0 / by, ALU.mult, ALU.add), after)
            t = V.do(lambda e: e.tensor_scalar(quotient, quotient, ROUND, ROUND, ALU.add, ALU.subtract), t)
            if remainder is None:
                return t
            return V.do(lambda e: e.scalar_tensor_tensor(remainder, quotient, -float(by), value, ALU.mult, ALU.add), t)

        def permute(out_rows, width, row, col, after, b, between=lambda j: None):
            used = [None] * 4
            for j in range(EJ):
                r, c = pick_row[j % 4], pick_col[j % 4]
                V.do(lambda e, j=j, r=r: e.tensor_scalar(r[R0, 0:out_rows], iota[R0, 0:out_rows], row[R0, j:j + 1], None, ALU.is_equal), after, used[j % 4])
                t = V.do(lambda e, j=j, c=c: e.tensor_scalar(c[R0, 0:width], iota[R0, 0:width], col[R0, j:j + 1], packed[R0, j:j + 1], ALU.is_equal, ALU.mult))
                used[j % 4] = T.do(lambda e, j=j, r=r, c=c: e.matmul(bank[0:out_rows, b, 0:width], r[R0, 0:out_rows], c[R0, 0:width], start=(j == 0), stop=(j == EJ - 1)), t)
                between(j)
            return used[(EJ - 1) % 4]

        t1 = V.do(lambda e: e.tensor_copy(src_g[R0, :], src_in[R0, :]), edges_in)
        t2 = V.do(lambda e: e.tensor_copy(dst_g[R0, :], dst_in[R0, :]))
        t3 = V.do(lambda e: e.tensor_scalar(digit_i[R0, :], dst_in[R0, :], LOW - 1, None, ALU.bitwise_and))
        V.do(lambda e: e.scalar_tensor_tensor(packed[R0, :], dst_g[R0, :], float(PACK), src_g[R0, :], ALU.mult, ALU.add), t1, t2)
        t4 = V.do(lambda e: e.tensor_copy(digit[R0, :], digit_i[R0, :]), t3)
        t = ranks(LOW, t4)
        low_ready = divide(place_hi[R0, :], place[R0, :], EJ, t, place_lo[R0, :])

        norm_turn = [0]

        def moments_of(rows_ap, *after):
            s = norm_turn[0] % 2
            norm_turn[0] += 1
            t = V.do(lambda e: e.bn_stats(stat[:, s, :], rows_ap), *after)
            t = V.do(lambda e: e.bn_aggr(moments[:, s, :], stat[:, s, :]), t)
            t = A.do(lambda e: e.activation(deviation[:, s, :], moments[:, s, 1:2], ACT.Sqrt, bias=eps[:, :]), t)
            return s, V.do(lambda e: e.reciprocal(rstd[:, s, :], deviation[:, s, :]), t)

        def normalise(out_ap, rows_ap, *after):
            s, t = moments_of(rows_ap, *after)
            return V.do(lambda e: e.tensor_scalar(out_ap, rows_ap, moments[:, s, 0:1], rstd[:, s, :], ALU.subtract, ALU.mult), t)

        def plain_relu(out_ap, rows_ap, *after):
            t = normalise(out_ap, rows_ap, *after)
            return V.do(lambda e: e.tensor_scalar(out_ap, out_ap, 0.0, None, ALU.max), t)

        def turn(rows_ap, b, dest, gain, offset, psum, *after):
            for k in range(KC):
                t = T.do(lambda e, k=k: e.transpose(bank[:, psum, k * P:(k + 1) * P], rows_ap[:, k * P:(k + 1) * P], ident[:, :]), *after)
            for k in range(KC):
                done = A.do(lambda e, k=k: e.activation(dest[:, k, b * P:(b + 1) * P], bank[:, psum, k * P:(k + 1) * P], ACT.Identity,
                                                        bias=column(offset, k), scale=column(gain, k)), t, columns_ready)
            return t, done

        t = V.do(lambda e: e.tensor_scalar(att_linear[:, :], att_relu[:, :], SLOPE, None, ALU.mult), wide_in)
        att_ready = V.do(lambda e: e.tensor_scalar(att_relu[:, :], att_relu[:, :], 1.0 - SLOPE, None, ALU.mult), t)
        wa_ready = None
        for side, w in ((0, w_left), (1, w_right)):
            s3 = scratch.rearrange("p (k n) -> p k n", n=D)
            t = V.do(lambda e, w=w: e.tensor_tensor(s3, w, over(att_linear[:, :], 1, KC), ALU.mult), att_ready, w_loaded, wa_ready)
            wa_ready = V.do(lambda e, side=side: e.tensor_reduce(wa[:, side, :, :].rearrange("p k h -> p (k h)"), scratch.rearrange("p (r c) -> p r c", c=C), AX.X, ALU.add), t)

        rows_read, turn_read, tile_free, tables_written = [None] * 2, [None] * 2, [None] * 4, []
        l_tile = [landing(f"tile{i}") for i in range(4)]
        bank_free = {}

        def project(b):
            h0 = plain_relu(state[:, b, :], x_in[:, b, :], x_loaded)
            t = normalise(rows[b % 2], state[:, b, :], h0, rows_read[b % 2])
            p = b % 2
            rows_read[b % 2], done = turn(rows[b % 2], b, trans, "L0_gnn_ln1_g", "L0_gnn_ln1_b", p, t, turn_read[p])
            turn_read[p] = done
            for side, (w, table) in enumerate(((w_left, left_table), (w_right, right_table))):
                n = 2 * b + side
                bk, small = 2 + side, 4
                o = (n % 4) * 16
                for k in range(KC):
                    lhs = trans[:, k, b * P:(b + 1) * P]
                    T.quiet(lambda e, k=k, w=w, lhs=lhs, bk=bk: e.matmul(bank[:, bk, :], lhs, w[:, k, :], start=(k == 0), stop=(k == KC - 1)), done, w_loaded, bank_free.get(bk))
                for k in range(KC):
                    lhs = trans[:, k, b * P:(b + 1) * P]
                    t = T.do(lambda e, k=k, side=side, lhs=lhs, o=side: e.matmul(bank[:, 4 + o, 0:HEADS], lhs, wa[:, side, k, :], start=(k == 0), stop=(k == KC - 1)), wa_ready)
                tl = tile[n % 4]
                A.do(lambda e, tl=tl, bk=bk: e.activation(tl[:, 0:D], bank[:, bk, :], ACT.Copy), t, tile_free[n % 4])
                bank_free[bk] = A.do(lambda e, tl=tl, side=side: e.activation(tl[:, D:TW], bank[:, 4 + side, 0:HEADS], ACT.Copy))
                tile_free[n % 4] = l_tile[n % 4].dma(S, lambda e, tl=tl, table=table, b=b: e.dma_start(table[b * P:(b + 1) * P, :], tl), bank_free[bk])
                tables_written.append(tile_free[n % 4])

        every = EJ // NB
        low_sorted = permute(EP, EJ, place_hi, place_lo, low_ready, 6,
                             lambda j: project(j // every) if j % every == 0 and j // every < NB else None)

        t = V.do(lambda e: e.tensor_copy(packed[R0, :], bank[R0, 6, 0:EJ]), low_sorted)
        t1 = V.do(lambda e: e.tensor_copy(digit_i[R0, :], packed[R0, :]), t)
        t1 = V.do(lambda e: e.tensor_scalar(digit_i[R0, :], digit_i[R0, :], (PACK * LOW).bit_length() - 1, None, ALU.arith_shift_right), t1)
        t1 = V.do(lambda e: e.tensor_copy(digit[R0, :], digit_i[R0, :]), t1)
        V.do(lambda e: e.tensor_scalar(packed[R0, :], packed[R0, :], float(PACK), None, ALU.add), t)
        zeroed = []

        def pad_blocks(after):
            t = T.do(lambda e: e.matmul(bank[:, 7, 0:HIGH], ones[R0, :], total[R0, 0:HIGH], start=True, stop=True), after, columns_ready)
            t = V.do(lambda e: e.tensor_copy(block_end, bank[:, 7, 0:HIGH].rearrange("p (b q) -> p b q", q=HPB)[:, :, HPB - 1]), t)
            t1 = V.do(lambda e: e.memset(block_before[:, 0:1], 0.0))
            t2 = V.do(lambda e: e.tensor_copy(block_before[:, 1:NB], block_end[:, 0:NB - 1]), t)
            t = V.do(lambda e: e.tensor_tensor(block_n, block_end, block_before, ALU.subtract), t1, t2)
            t = V.do(lambda e: e.tensor_scalar(block_n, block_n, float(PAIR - 1), None, ALU.add), t)
            t = divide(pairs, block_n, PAIR, t)
            t = V.do(lambda e: e.tensor_tensor_scan(pair_end, pairs, pairs, 0.0, ALU.add, ALU.max), t)
            t = V.do(lambda e: e.tensor_tensor(pair_at, pair_end, pairs, ALU.subtract), t)
            t = V.do(lambda e: e.scalar_tensor_tensor(shift, pair_at, float(PAIR), block_before, ALU.mult, ALU.subtract), t)
            b3 = base_of[R0, 0:HIGH].rearrange("p (b q) -> p b q", q=HPB)
            out_t = V.do(lambda e: e.tensor_tensor(b3, b3, over(shift[R0, :], 2, HPB), ALU.add), t)
            p3 = passed.rearrange("p (g b) -> p g b", b=NB - 1)
            t = V.do(lambda e: e.tensor_tensor(p3, over(pair_at[:, 1:NB], 1, NG), over(iota[:, 0:NG], 2, NB - 1), ALU.is_le), t)
            t = V.do(lambda e: e.tensor_reduce(block_f, p3, AX.X, ALU.add), t)
            zeroed.append(V.do(lambda e: e.tensor_copy(block_of[:, :], block_f[0:1, :]), t))
            return out_t

        t = ranks(HIGH, t1, pad_blocks)
        high_ready = divide(place_hi[R0, :], place[R0, :], P, t, place_lo[R0, :])
        t = permute(P, NC, place_lo, place_hi, high_ready, 6)
        t = V.do(lambda e: e.tensor_copy(slots_i, bank[:, 6, 0:NC]), t)
        V.do(lambda e: e.tensor_scalar(src_of[:, :], slots_i, PACK - 1, None, ALU.bitwise_and), t)
        t1 = V.do(lambda e: e.tensor_scalar(part_i, slots_i, PACK.bit_length() - 1, None, ALU.arith_shift_right))
        V.do(lambda e: e.tensor_copy(src_f[:, :], src_of[:, :]), t1)
        t = V.do(lambda e: e.tensor_copy(key[:, :], part_i), t1)
        V.do(lambda e: e.tensor_scalar(dst_of[:, :], key[:, :], -1.0, 0.0, ALU.add, ALU.max), t)
        l3 = local[:, :].rearrange("p (g i) -> p g i", i=2)
        t = V.do(lambda e: e.scalar_tensor_tensor(l3, over(block_f, 2, 2), -float(P), key[:, :].rearrange("p (g i) -> p g i", i=2), ALU.mult, ALU.add), t)
        slots_ready = V.do(lambda e: e.tensor_scalar(local[:, :], local[:, :], -1.0, None, ALU.add), t)
        t_zero = V.do(lambda e: e.memset(counts[:, :, :], 0.0), slots_ready)
        block_ready = slots_ready

        DEPTH = 6
        plan = Plan(0)
        gathered = [plan.take(2, TW) for _ in range(DEPTH)]
        weighted = [plan.take(2, D) for _ in range(2)]
        score = plan.take(NC, HEADS)
        hot_at = plan.at
        src_hot = [plan.take(NP, dt=BF16) for _ in range(4)]
        dst_hot = [plan.take(P, dt=BF16) for _ in range(4)]
        hot_end = plan.at
        weights = plan.take(NC, HEADS + 1)
        hot = [plan.take(P) for _ in range(4)]
        agg_at = plan.at
        agg = plan.take(NB, D)
        agg_den = plan.take(NB, HEADS + 1)
        phase_end = plan.at
        w1_at = SIZE - KC * F
        assert phase_end <= w1_at, (phase_end, w1_at)
        w1 = Plan(w1_at).take(KC, F)
        l_w1 = landing("w1")
        w1_loaded = l_w1.dma(S, lambda e: e.dma_start(w1, w_view(ins["L0_gnn_W1"])), high_ready, t)

        ones_ready = V.do(lambda e: e.memset(weights[:, :, HEADS], 1.0), *tables_written[-4:])

        l_gather = [landing(f"gather{i}") for i in range(DEPTH)]
        l_add = [landing(f"add{i}") for i in range(DEPTH)]
        gather_free = [ones_ready] * DEPTH
        own = [None] * DEPTH

        def gather(lands, table, index, g, i, add, *after):
            extra = dict(compute_op=ALU.add, bounds_check=NP - 1, oob_is_err=True) if add else {}
            c = 2 * g + i
            return lands.dma(G, lambda e: e.indirect_dma_start(
                out=gathered[g % DEPTH][:, i, :], out_offset=None, in_=table,
                in_offset=bass.IndirectOffsetOnAxis(ap=index[:, c:c + 1], axis=0), **extra), *after)

        def gather_left(g):
            for i in range(2):
                own[g % DEPTH] = gather(l_gather[g % DEPTH], left_table, src_of, g, i, False, slots_ready, gather_free[g % DEPTH], *tables_written[-4:])

        AHEAD = 3
        weighted_free, hot_free, count_free = [None] * 2, [None] * 4, [t_zero] * 2
        counted = [None] * 2
        block_reg = {}

        def count_pair(g):
            lo = 3 * (g % 2)
            for i in range(2):
                c = 2 * g + i
                s = c % 4
                V.do(lambda e, c=c, s=s: e.tensor_scalar(src_hot[s], iota_node[:, :], src_f[:, c:c + 1], None, ALU.is_equal), hot_free[s])
                t = V.do(lambda e, c=c, s=s: e.tensor_scalar(dst_hot[s], iota_node[:, 0:P], local[:, c:c + 1], None, ALU.is_equal))
                for b in range(NB):
                    o = flat[:, lo * 512 + b * P:lo * 512 + (b + 1) * P]
                    f = lambda e, s=s, b=b, o=o, i=i: e.matmul(o, src_hot[s][:, b * P:(b + 1) * P], dst_hot[s], start=(i == 0 and b % 4 == 0), stop=(i == 1), skip_group_check=True)
                    if b < NB - 1:
                        T.quiet(f, t, count_free[g % 2])
                    else:
                        hot_free[s] = T.do(f)
            return hot_free[(2 * g + 1) % 4]

        def at_block(g, fn):
            def emit(e):
                r = e.value_load(block_of[0:1, g:g + 1], min_val=0, max_val=NB - 1)
                return fn(e, r)
            return emit

        def add_counts(g, ready):
            lo = 3 * (g % 2)

            def fn(e, r):
                d = counts[:, :, bass.ds(r * P, P)]
                return e.tensor_tensor(d, d, flat[:, lo * 512:lo * 512 + NP].rearrange("p (b n) -> p b n", n=P), ALU.add)
            count_free[g % 2] = V.do(at_block(g, fn), ready, block_ready, count_free[(g + 1) % 2])

        for g in range(AHEAD):
            gather_left(g)
        ready_counts = None
        for g in range(NG):
            s = g % DEPTH
            if g + AHEAD < NG:
                gather_left(g + AHEAD)
            for i in range(2):
                t = gather(l_add[s], right_table, dst_of, g, i, True, own[s])
            counted_now = count_pair(g)
            w = weighted[g % 2]
            t1 = V.do(lambda e, s=s, w=w: e.scalar_tensor_tensor(w, gathered[s][:, :, 0:D], 0.0, over(att_relu[:, :], 1, 2), ALU.max, ALU.mult), t, weighted_free[g % 2])
            sc = score[:, 2 * g:2 * g + 2, :]
            t1 = V.do(lambda e, w=w, sc=sc: e.tensor_reduce(sc.rearrange("p i h -> p (i h)"), w.rearrange("p i (h c) -> p (i h) c", c=C), AX.X, ALU.add), t1)
            weighted_free[g % 2] = t1
            gather_free[s] = V.do(lambda e, s=s, sc=sc: e.tensor_tensor(sc, sc, gathered[s][:, :, D:TW], ALU.add), t1)
            if g:
                add_counts(g - 1, ready_counts)
            ready_counts = counted_now
        add_counts(NG - 1, ready_counts)
        scores_ready = gather_free[(NG - 1) % DEPTH]

        plan = Plan(hot_at, hot_end)
        key_rows = plan.take(SK, P)
        turned_key = plan.take(RUN)
        plan = Plan(agg_at, phase_end)
        reset = plan.take(RUN)
        ahead_max = plan.take(RUN)
        turned = plan.take(RUN)
        ends = plan.take(4 * SG)
        small = plan.take(12 * SG)
        carry_rows = plan.take(2 * SG)
        carry = plan.take(2)
        behind_max = key_rows.rearrange("p k n -> p (k n)")
        by_run = lambda ap: ap.rearrange("p (g k) h -> p g k h", k=SK)
        k4 = key_rows.rearrange("p k (g h) -> p k g h", h=HEADS)
        kk = key[:, :].rearrange("p (g k) -> p k g", k=SK)
        t = V.do(lambda e: e.tensor_copy(k4, over(kk, 3, HEADS)), hot_free[0], hot_free[1], hot_free[2], hot_free[3])
        score_rows = [Plan(DEPTH * 2 * TW).take(SK, P)][0]
        t2 = V.do(lambda e: e.tensor_copy(score_rows.rearrange("p k (g h) -> p k g h", h=HEADS), by_run(score).rearrange("p g k h -> p k g h")), scores_ready)
        for k in range(SK):
            T.quiet(lambda e, k=k: e.transpose(flat[:, k * P:(k + 1) * P], key_rows[:, k, :], ident[:, :]), t, t2, count_free[0], count_free[1])
        tk = T.do(lambda e: e.transpose(flat[:, 1536:1536 + P], score_rows[:, 0, :], ident[:, :]))
        for k in range(1, SK):
            ts = T.do(lambda e, k=k: e.transpose(flat[:, 1536 + k * P:1536 + (k + 1) * P], score_rows[:, k, :], ident[:, :]))
        t1 = V.do(lambda e: e.tensor_copy(turned_key, flat[:, 0:RUN]), tk)
        t2 = V.do(lambda e: e.tensor_copy(turned, flat[:, 1536:1536 + RUN]), ts)
        t3 = V.do(lambda e: e.memset(reset[:, 0:1], 0.0))
        t4 = V.do(lambda e: e.tensor_tensor(reset[:, 1:RUN], turned_key[:, 1:RUN], turned_key[:, 0:RUN - 1], ALU.not_equal), t1)
        t4 = V.do(lambda e: e.tensor_scalar(reset[:, 1:RUN], reset[:, 1:RUN], FAR, None, ALU.mult), t4)
        t5 = V.do(lambda e: e.tensor_tensor_scan(ahead_max, reset, turned, FAR, ALU.add, ALU.max), t2, t3, t4)
        t6 = V.do(lambda e: e.tensor_copy(behind_max[:, RUN - 1:RUN], turned[:, RUN - 1:RUN]), ts)
        t7 = V.do(lambda e: e.tensor_tensor_scan(behind_max[:, 0:RUN - 1][:, ::-1], reset[:, 1:RUN][:, ::-1], turned[:, 0:RUN - 1][:, ::-1],
                                                 turned[:, RUN - 1:RUN], ALU.add, ALU.max), t6)
        for n, col in enumerate((ahead_max[:, RUN - 1:RUN], behind_max[:, 0:1], turned_key[:, 0:1], turned_key[:, RUN - 1:RUN])):
            t = V.do(lambda e, n=n, col=col: e.tensor_scalar(ends[:, n * SG:(n + 1) * SG], is_run[:, :], col, None, ALU.mult), t5, t7, t1)
        t = T.do(lambda e: e.matmul(bank[0:HEADS, 6, 0:4 * SG], is_head[:, :], ends, start=True, stop=True), t)
        H8 = slice(0, HEADS)
        sm = [small[H8, i * SG:(i + 1) * SG] for i in range(12)]
        t = V.do(lambda e: e.tensor_copy(small[H8, 0:4 * SG], bank[0:HEADS, 6, 0:4 * SG]), t)
        right_end, left_end, first_key, last_key, wall, wall_b, over_f, over_b, chain_f, chain_b = sm[0:10]
        carry_f, carry_b = carry_rows[H8, 0:SG], carry_rows[H8, SG:2 * SG]

        def walls(dest, one, other, *after):
            t = V.do(lambda e: e.tensor_tensor(dest, one, other, ALU.not_equal), *after)
            return V.do(lambda e: e.tensor_scalar(dest, dest, FAR, None, ALU.mult), t)
        V.do(lambda e: e.memset(small[H8, 4 * SG:8 * SG], 0.0))
        t0 = V.do(lambda e: e.memset(carry_rows[H8, :], FAR))
        ta = walls(wall[:, 1:SG], last_key[:, 1:SG], last_key[:, 0:SG - 1], t, t0)
        tb = walls(wall_b[:, 0:SG - 1], first_key[:, 0:SG - 1], first_key[:, 1:SG])
        tc = walls(over_f[:, 1:SG], first_key[:, 1:SG], last_key[:, 0:SG - 1])
        ta = V.do(lambda e: e.tensor_tensor_scan(chain_f, wall, right_end, FAR, ALU.add, ALU.max), ta)
        tb = V.do(lambda e: e.tensor_tensor_scan(chain_b[:, ::-1], wall_b[:, ::-1], left_end[:, ::-1], FAR, ALU.add, ALU.max), tb)
        V.do(lambda e: e.tensor_tensor(carry_f[:, 1:SG], chain_f[:, 0:SG - 1], over_f[:, 1:SG], ALU.add), ta, tc)
        t = V.do(lambda e: e.tensor_tensor(carry_b[:, 0:SG - 1], chain_b[:, 1:SG], over_f[:, 1:SG], ALU.add), tb)
        t = T.do(lambda e: e.matmul(bank[:, 6, 128:128 + 2 * SG], to_rows[:, :], carry_rows[H8, :], start=True, stop=True), t)
        c3 = ends[:, 0:2 * SG].rearrange("p (w g) -> p w g", w=2)
        t = V.do(lambda e: e.tensor_tensor(c3, bank[:, 6, 128:128 + 2 * SG].rearrange("p (w g) -> p w g", w=2), over(is_run[:, :], 1, 2), ALU.mult), t)
        t = V.do(lambda e: e.tensor_reduce(carry, c3, AX.X, ALU.add), t)
        t1 = V.do(lambda e: e.tensor_scalar(reset, turned_key, turned_key[:, 0:1], FAR, ALU.not_equal, ALU.mult), t5)
        m1 = V.do(lambda e: e.scalar_tensor_tensor(ahead_max, reset, carry[:, 0:1], ahead_max, ALU.add, ALU.max), t, t1)
        t1 = V.do(lambda e: e.tensor_scalar(reset, turned_key, turned_key[:, RUN - 1:RUN], FAR, ALU.not_equal, ALU.mult), m1)
        m2 = V.do(lambda e: e.scalar_tensor_tensor(behind_max, reset, carry[:, 1:2], behind_max, ALU.add, ALU.max), t1)
        t = V.do(lambda e: e.tensor_tensor(ahead_max, ahead_max, behind_max, ALU.max), m2)
        t = V.do(lambda e: e.tensor_tensor(turned, turned, ahead_max, ALU.subtract), t)
        t = A.do(lambda e: e.activation(turned, turned, ACT.Exp), t)
        for k in range(SK):
            tw = T.do(lambda e, k=k: e.transpose(flat[:, k * P:(k + 1) * P], turned[:, k * P:(k + 1) * P], ident[:, :]), t)
        w4 = weights[:, :, 0:HEADS].rearrange("p (g k) h -> p k g h", k=SK)
        weights_ready = V.do(lambda e: e.tensor_copy(w4, flat[:, 0:RUN].rearrange("p (k g h) -> p k g h", g=SG, h=HEADS)), tw, ones_ready)

        l_again = [landing(f"again{i}") for i in range(DEPTH)]
        free = [gather_free[(NG - 1 - (NG - 1 - i) % DEPTH) % DEPTH] for i in range(DEPTH)]
        landed = [None] * DEPTH

        def gather_again(g):
            for i in range(2):
                landed[g % DEPTH] = gather(l_again[g % DEPTH], left_table, src_of, g, i, False, free[g % DEPTH])
        for g in range(DEPTH - 1):
            gather_again(g)
        G.do(lambda e: e.memset(agg, 0.0), tw)
        agg_zero = G.do(lambda e: e.memset(agg_den, 0.0))
        hot_free = [None] * 4
        weighted_free = [weights_ready] * 2
        sum_free = [agg_zero] * 2
        pending = None

        def add_sums(g, ready):
            b0 = g % 2

            def fn(e, r):
                d = agg[:, bass.ds(r, 1), :].rearrange("p b n -> p (b n)")
                return e.tensor_tensor(d, d, bank[:, b0, :], ALU.add)

            def fn_den(e, r):
                d = agg_den[:, bass.ds(r, 1), :].rearrange("p b n -> p (b n)")
                return e.tensor_tensor(d, d, bank[:, 2 + b0, 0:HEADS + 1], ALU.add)
            last = sum_free[(g + 1) % 2]

            def both(e):
                r = e.value_load(block_of[0:1, g:g + 1], min_val=0, max_val=NB - 1)
                fn(e, r).then_inc(V.sem, 1)
                return fn_den(e, r)
            V.count += 1
            sum_free[g % 2] = V.do(both, ready, last)

        for g in range(NG):
            s = g % DEPTH
            w = weighted[g % 2]
            t = V.do(lambda e, s=s, w=w, g=g: e.tensor_tensor(
                w.rearrange("p i (h c) -> p i h c", c=C), gathered[s][:, :, 0:D].rearrange("p i (h c) -> p i h c", c=C),
                over(weights[:, 2 * g:2 * g + 2, 0:HEADS], 3, C), ALU.mult), landed[s], weighted_free[g % 2], weights_ready)
            free[s] = t
            if g + DEPTH - 1 < NG:
                gather_again(g + DEPTH - 1)
            for i in range(2):
                c = 2 * g + i
                h = hot[c % 4]
                t = V.do(lambda e, h=h, c=c: e.tensor_scalar(h, iota[:, 0:P], local[:, c:c + 1], None, ALU.is_equal), hot_free[c % 4])
                T.quiet(lambda e, h=h, w=w, i=i, g=g: e.matmul(bank[:, g % 2, :], h, w[:, i, :], start=(i == 0), stop=(i == 1)), t, sum_free[g % 2])
                hot_free[c % 4] = T.do(lambda e, h=h, c=c, i=i, g=g: e.matmul(bank[:, 2 + g % 2, 0:HEADS + 1], h, weights[:, c, :], start=(i == 0), stop=(i == 1)))
            weighted_free[g % 2] = hot_free[(2 * g + 1) % 4]
            if pending:
                add_sums(*pending)
            pending = (g, hot_free[(2 * g + 1) % 4])
        add_sums(*pending)
        sums_done = sum_free[(NG - 1) % 2]

        t = V.do(lambda e: e.tensor_reduce(norm_src[:, :], counts[:, :, :], AX.X, ALU.add), count_free[0], count_free[1], sums_done)
        t1 = V.do(lambda e: e.tensor_scalar(norm_src[:, :], norm_src[:, :], 1.0, None, ALU.max), t)
        t2 = V.do(lambda e: e.tensor_scalar(norm_dst[:, :], agg_den[:, :, HEADS], 1.0, None, ALU.max))
        A.do(lambda e: e.activation(norm_src[:, :], norm_src[:, :], ACT.Sqrt), t1)
        t = A.do(lambda e: e.activation(norm_dst[:, :], norm_dst[:, :], ACT.Sqrt), t2)
        V.do(lambda e: e.reciprocal(norm_src[:, :], norm_src[:, :]), t)
        norms_ready = V.do(lambda e: e.reciprocal(norm_dst[:, :], norm_dst[:, :]))

        plan = Plan(0)
        w2 = plan.take(FC, D)
        assert plan.at <= w1_at
        hid_plan = Plan(plan.at)
        trans2 = hid_plan.take(KC, NP)
        hid_at = hid_plan.at
        l_w2 = landing("w2")
        hidden = Plan(hid_at).take(FC, GROUP * P)
        rows2 = [Plan(SIZE - KC * F - D * (1 + i)).take(D) for i in range(2)]
        assert hid_at + FC * GROUP * P <= w1_at - 2 * D, (hid_at, w1_at)

        t = V.do(lambda e: e.tensor_scalar(agg_den, agg_den, 1e-16, None, ALU.add), sums_done, t2)
        t = V.do(lambda e: e.reciprocal(agg_den, agg_den), t)
        for b in range(NB):
            a3 = agg[:, b, :].rearrange("p (h c) -> p h c", c=C)
            t1 = V.do(lambda e, b=b, a3=a3: e.tensor_tensor(a3, a3, over(agg_den[:, b, 0:HEADS], 2, C), ALU.mult), t)
            V.do(lambda e, b=b: e.tensor_tensor(state[:, b, :], state[:, b, :], gat_bias[:, :], ALU.add))
            x1_ready = V.do(lambda e, b=b: e.tensor_tensor(state[:, b, :], state[:, b, :], agg[:, b, :], ALU.add), t1, (V.sem, V.count))
        w2_loaded = l_w2.dma(S, lambda e: e.dma_start(w2, ins["L0_gnn_W2"].rearrange("(k p) n -> p k n", p=P)), x1_ready, weighted_free[(NG - 1) % 2])
        rows_read = [None] * 2
        turned_b = [None] * NB
        turn_free = [sums_done] * 2
        for b in range(NB):
            t = normalise(rows2[b % 2], state[:, b, :], x1_ready, rows_read[b % 2])
            rows_read[b % 2], done = turn(rows2[b % 2], b, trans2, "L0_gnn_ln2_g", "L0_gnn_ln2_b", b % 2, t, turn_free[b % 2])
            turn_free[b % 2] = done
            turned_b[b] = done
        x_again = [Plan(w1_at - 2 * D).take(D), Plan(w1_at - D).take(D)]
        l_x2 = [landing("x_again0"), landing("x_again1")]
        again_free = [rows_read[1], rows_read[0]]
        again_free = [turned_b[NB - 1], turned_b[NB - 1]]
        for b in range(NB):
            n = P if b < NB - 1 else LAST
            ta = V.do(lambda e, b=b: e.tensor_tensor(state[:, b, :], state[:, b, :], b2[:, :], ALU.add), turned_b[NB - 1])
            ld = l_x2[b % 2].dma(S, lambda e, b=b, n=n: e.dma_start(x_again[b % 2][0:n, :], ins["x"][b * P:b * P + n, :]), again_free[b % 2])
            again_free[b % 2] = rest_ready = V.do(lambda e, b=b, n=n: e.tensor_tensor(state[0:n, b, :], state[0:n, b, :], x_again[b % 2][0:n, :], ALU.add), ld, ta)

        hid_free = [None] * 2
        out_free = [None] * GROUP
        x2_ready = [None] * NB
        for g0 in range(0, NB, GROUP):
            nb = min(GROUP, NB - g0)
            cols = min(nb * P, N - g0 * P)
            for f in range(FC):
                for k in range(KC):
                    t = T.do(lambda e, f=f, k=k, g0=g0, cols=cols: e.matmul(bank[:, f % 2, 0:cols], w1[:, k, f * P:(f + 1) * P], trans2[:, k, g0 * P:g0 * P + cols], start=(k == 0), stop=(k == KC - 1)),
                             w1_loaded, turned_b[NB - 1], hid_free[f % 2])
                hid_free[f % 2] = A.do(lambda e, f=f, cols=cols: e.activation(hidden[:, f, 0:cols], bank[:, f % 2, 0:cols], ACT.Gelu, bias=column("L0_gnn_b1", f)), t, sums_done)
            for q in range(nb):
                b = g0 + q
                n = min(P, N - b * P)
                for f in range(FC):
                    t = T.do(lambda e, f=f, q=q, n=n: e.matmul(bank[0:n, 2 + q, :], hidden[:, f, q * P:q * P + n], w2[:, f, :], start=(f == 0), stop=(f == FC - 1)),
                             hid_free[(FC - 1) % 2], w2_loaded, out_free[q])
                out_free[q] = x2_ready[b] = V.do(lambda e, b=b, q=q, n=n: e.tensor_tensor(state[0:n, b, :], state[0:n, b, :], bank[0:n, 2 + q, :], ALU.add), t, rest_ready)
        mlp_done = t

        plan = Plan(0)
        layer_w = plan.take(LAYERS, KC, D)
        trans3 = plan.take(KC, NP)
        hw = plan.take(NB, D)
        h = plan.take(NB, D)
        rows3 = [plan.take(D) for _ in range(2)]
        l_lw = [landing(f"layer_w{i}") for i in range(LAYERS)]
        lw = [l_lw[i].dma(S, lambda e, i=i: e.dma_start(layer_w[:, i, :, :], w_view(ins["L1_gnn_W"][i, :, :])), mlp_done) for i in range(LAYERS)]
        h_ready = [plain_relu(h[:, b, :], state[:, b, :], x2_ready[b], mlp_done) for b in range(NB)]
        rows_read = [None] * 2
        turn_free = [x2_ready[NB - 1]] * 2
        mul_free = [x2_ready[NB - 1]] * 2
        agg_free = [x2_ready[NB - 1]] * 2
        l_out = landing("out")
        last_agg = None
        for i in range(LAYERS):
            hw_ready = [None] * NB
            for b in range(NB):
                t = normalise(rows3[b % 2], h[:, b, :], h_ready[b], rows_read[b % 2])
                psum = b % 2
                for k in range(KC):
                    t = T.do(lambda e, k=k, b=b, psum=psum: e.transpose(bank[:, psum, k * P:(k + 1) * P], rows3[b % 2][:, k * P:(k + 1) * P], ident[:, :]), t, turn_free[psum])
                rows_read[b % 2] = t
                for k in range(KC):
                    done = A.do(lambda e, k=k, b=b, i=i, psum=psum: e.activation(trans3[:, k, b * P:(b + 1) * P], bank[:, psum, k * P:(k + 1) * P], ACT.Identity,
                                bias=column("L1_gnn_ln_b", i * KC + k), scale=column("L1_gnn_ln_g", i * KC + k)), t)
                turn_free[psum] = done
                for k in range(KC):
                    t = T.do(lambda e, k=k, b=b, i=i: e.matmul(bank[:, 2 + b % 2, :], trans3[:, k, b * P:(b + 1) * P], layer_w[:, i, k, :], start=(k == 0), stop=(k == KC - 1)),
                             done, lw[i], mul_free[b % 2])
                mul_free[b % 2] = hw_ready[b] = A.do(lambda e, b=b: e.activation(hw[:, b, :], bank[:, 2 + b % 2, :], ACT.Copy, scale=norm_src[:, b:b + 1]), t, norms_ready, last_agg)
            for b in range(NB):
                n = min(P, N - b * P)
                for s in range(NB):
                    t = T.do(lambda e, b=b, s=s, n=n: e.matmul(bank[0:n, 4 + b % 2, :], counts[:, s, b * P:b * P + n], hw[:, s, :], start=(s == 0), stop=(s == NB - 1)),
                             hw_ready[s], agg_free[b % 2])
                agg_free[b % 2] = t = V.do(lambda e, b=b, i=i, n=n: e.scalar_tensor_tensor(h[0:n, b, :], bank[0:n, 4 + b % 2, :], norm_dst[0:n, b:b + 1], layer_bias[0:n, i, :], ALU.mult, ALU.add), t)
                if i < LAYERS - 1:
                    h_ready[b] = V.do(lambda e, b=b, n=n: e.tensor_scalar(h[0:n, b, :], h[0:n, b, :], 0.0, None, ALU.max), t)
                else:
                    t = V.do(lambda e, b=b, n=n: e.tensor_tensor(h[0:n, b, :], h[0:n, b, :], state[0:n, b, :], ALU.add), t)
                    l_out.dma(S, lambda e, b=b, n=n: e.dma_start(out[b * P:b * P + n, :], h[0:n, b, :]), t)
            last_agg = (T.sem, T.count)

        for l in landings:
            S.wait((l.sem, l.count))
        with nc.Block() as block:
            block.vector(V.run)
            block.scalar(A.run)
            block.tensor(T.run)
            block.gpsimd(G.run)
            block.sync(S.run)


_INS = ['x', 'src', 'dst', 'L0_gnn_ln1_g', 'L0_gnn_ln1_b', 'L0_gnn_Wl', 'L0_gnn_Wr', 'L0_gnn_att', 'L0_gnn_gat_bias',
        'L0_gnn_ln2_g', 'L0_gnn_ln2_b', 'L0_gnn_W1', 'L0_gnn_b1', 'L0_gnn_W2', 'L0_gnn_b2', 'L1_gnn_ln_g', 'L1_gnn_ln_b',
        'L1_gnn_W', 'L1_gnn_b']


def kernel(**inputs):
    import numpy as _np
    import concourse.bacc as _bacc
    from concourse import mybir as _mybir
    from concourse.bass_utils import run_bass_kernel_spmd as _run

    nc = _bacc.Bacc("TRN2", target_bir_lowering=False, num_devices=1)
    arrays, args = {}, {}
    for name in _INS:
        a = _np.ascontiguousarray(inputs[name])
        arrays[f"in_{name}_dram"] = a
        args[name] = nc.dram_tensor(f"in_{name}_dram", a.shape, _mybir.dt.from_np(a.dtype), kind="ExternalInput").ap()
    out = nc.dram_tensor("out_0_dram", args["x"].shape, _mybir.dt.float32, kind="ExternalOutput").ap()
    build(nc, args, out)
    r = _run(nc, [arrays], core_ids=[0])
    return r.results[0]["out_0_dram"]
```

```python
from contextlib import ExitStack

import concourse.bass as bass
from concourse import mybir

ALU = mybir.AluOpType
ACT = mybir.ActivationFunctionType
AX = mybir.AxisListType
F32 = mybir.dt.float32
BF16 = mybir.dt.bfloat16
FP16 = mybir.dt.float16
I32 = mybir.dt.int32
F32R = mybir.dt.float32r

P = 128
ROUND = 1.5 * 2.0 ** 23
EXACT = 4096.0
FAR = -1.0e30
LN_EPS = 1e-5
SLOPE = 0.2


class Queue:

    def __init__(self, sem):
        self.sem, self.count, self.ops, self.seen = sem, 0, [], {}

    def wait(self, *after):
        for token in after:
            if token is None:
                continue
            sem, value = token
            if self.seen.get(id(sem), 0) < value:
                self.seen[id(sem)] = value
                self.ops.append(lambda e, sem=sem, value=value: e.wait_ge(sem, value))

    def do(self, fn, *after):
        self.wait(*after)
        self.count += 1
        self.ops.append(lambda e: fn(e).then_inc(self.sem, 1))
        return (self.sem, self.count)

    def quiet(self, fn, *after):
        self.wait(*after)
        self.ops.append(fn)

    def run(self, engine):
        for op in self.ops:
            op(engine)


class Landing:

    def __init__(self, sem):
        self.sem, self.count = sem, 0

    def dma(self, queue, fn, *after):
        queue.wait(*after)
        self.count += 16
        queue.ops.append(lambda e: fn(e).then_inc(self.sem, 16))
        return (self.sem, self.count)


def build(nc, ins, out):
    N, D = ins["x"].shape
    E = ins["src"].shape[0]
    HEADS, C = ins["L0_gnn_att"].shape
    F = ins["L0_gnn_W1"].shape[1]
    LAYERS = ins["L1_gnn_W"].shape[0]
    NB = -(-N // P)
    NP = NB * P
    LAST = N - (NB - 1) * P
    KC = D // P
    FC = F // P
    EP = 125
    EJ = E // EP
    LOW = 32
    HIGH = NP // LOW
    HPB = P // LOW
    PACK = 2048
    PAIR = 2 * P
    NG = (E + NB * (PAIR - 1)) // PAIR
    NC = 2 * NG
    TW = D + HEADS
    SG = P // HEADS
    SK = NC // SG
    RUN = SK * P
    GROUP = 4
    VECTORS = KC * (4 + 2 * LAYERS) + FC
    assert E == EP * EJ and N < PACK and SG * SK == NC and NP % LOW == 0

    with ExitStack() as ctx:
        sem = lambda n: ctx.enter_context(nc.semaphore(n))
        V, A, T, G, S = [Queue(sem("s_" + n)) for n in ("vector", "scalar", "tensor", "gpsimd", "sync")]
        landings = []

        def landing(name):
            landings.append(Landing(sem("d_" + name)))
            return landings[-1]

        def sb(name, shape, dt=F32):
            return ctx.enter_context(nc.sbuf_tensor(name, shape, dt))

        left_table = nc.dram_tensor("left_table", (NP, TW), F32, kind="Internal").ap()
        right_table = nc.dram_tensor("right_table", (NP, TW), F32, kind="Internal").ap()

        bank = ctx.enter_context(nc.psum_tensor("bank", [P, 8, 512], F32))
        flat = bank[:, :, :].rearrange("p b n -> p (b n)")

        ident = sb("ident", [P, P])
        ones = sb("ones", [P, P])
        earlier = sb("earlier", [P, P])
        iota = sb("iota", [P, max(NC, EJ)])
        is_head = sb("is_head", [P, HEADS])
        is_run = sb("is_run", [P, SG])
        to_rows = sb("to_rows", [HEADS, P])
        columns = sb("columns", [P, VECTORS])
        b2 = sb("b2", [P, D])
        eps = sb("eps", [P, 1])
        zero = sb("zero", [P, 1])
        state = sb("state", [P, NB, D])
        block_of = sb("block_of", [1, NG], I32)
        exact_flag = sb("exact_flag", [1, 1], I32)
        most = sb("most", [P, 1])
        most_row = sb("most_row", [1, 1])
        norm_slots = NB + 2
        stat = sb("stat", [P, norm_slots, 6])
        moments = sb("moments", [P, norm_slots, 2])
        deviation = sb("deviation", [P, norm_slots, 1])
        rstd = sb("rstd", [P, norm_slots, 1])
        norm_src = sb("norm_src", [P, NB])
        norm_dst = sb("norm_dst", [P, NB])
        aligned = lambda at: -(-at // 32) * 32
        counts_at = aligned(nc.sbuf_base)
        counts = sb("counts", [P, NB, NP])
        counts_r = nc.alloc_sbuf_tensor_at("counts_r", [P, NB, NP], F32R, offset=counts_at)
        arena_at = aligned(nc.sbuf_base)
        SIZE = (nc.sbuf_usable_end - arena_at) // 32 * 8
        arena = sb("arena", [P, SIZE])

        class Plan:

            def __init__(self, at, end=SIZE, base=arena):
                self.at, self.end, self.base = at, end, base

            def room(self, words):
                assert self.at + words <= self.end, (self.at, words, self.end)
                self.at += words
                return self.at - words

            def take(self, *shape, dt=F32):
                size = 1
                for n in shape:
                    size *= n
                words = size if dt in (F32, I32) else -(-size // 2)
                at = self.room(words)
                ap = self.base[:, at:at + words]
                if dt is not F32:
                    ap = ap.bitcast(dt)
                if len(shape) > 1:
                    names = " ".join(f"a{i}" for i in range(len(shape)))
                    ap = ap.rearrange(f"p ({names}) -> p {names}", **{f"a{i}": n for i, n in enumerate(shape)})
                return ap

            def rounded(self, name, *shape):
                size = 1
                for n in shape:
                    size *= n
                at = self.room(size)
                t = nc.alloc_sbuf_tensor_at(name, [P, *shape], F32R, offset=arena_at + 4 * at)
                return t[(slice(None),) * (1 + len(shape))]

        def over(ap, axis, n):
            shape = list(ap.shape)
            shape.insert(axis, n)
            return ap.unsqueeze(axis).broadcast_to(shape)

        W1_AT = SIZE - KC * F
        w1 = Plan(W1_AT).take(KC, F)
        EARLY = 2900
        plan = Plan(W1_AT - EARLY, W1_AT)
        iota_node = plan.take(NP, dt=FP16)
        gat_bias = plan.take(D)
        src_of, dst_of = plan.take(NC, dt=I32), plan.take(NC, dt=I32)
        src_f = plan.take(NC)
        key = plan.take(NC)
        local = plan.take(NC)
        minus_local = plan.take(NC)
        att_relu = plan.take(D)

        plan = Plan(0, W1_AT - EARLY)
        x_in = plan.take(NB, D)
        trans = [plan.take(KC, P) for _ in range(3)]
        w_left = plan.take(KC, D)
        w_right = plan.take(KC, D)
        wa = plan.take(2, KC, HEADS)
        tile = [plan.take(TW) for _ in range(4)]
        scratch = plan.take(KC * D)
        ranked = plan.take(HIGH * EJ)
        sort = Plan(0, NB * NP, counts[:, :, :].rearrange("p b n -> p (b n)"))
        digit = sort.take(EJ, dt=BF16)
        digits = sort.take(HIGH, EJ, dt=BF16)
        match = sort.take(HIGH * EJ, dt=BF16)
        running = sort.take(HIGH * EJ, dt=BF16)
        src_in, dst_in, digit_i = sort.take(EJ, dt=I32), sort.take(EJ, dt=I32), sort.take(EJ, dt=I32)
        src_g, dst_g, packed, place, place_hi, place_lo = [sort.take(EJ) for _ in range(6)]
        total, shifted, per_digit, base_of = [sort.take(HIGH) for _ in range(4)]
        block_end, block_before, block_n, pairs, pair_end, pair_at, shift = [sort.take(NB) for _ in range(7)]
        columns_in = sort.take(P)
        RING = 6
        rings = Plan(0, HIGH * EJ, ranked)
        pick_row = [rings.take(P) for _ in range(RING)]
        pick_col = [rings.take(max(NC, EJ)) for _ in range(RING)]
        late = Plan(0, KC * D, scratch)
        passed, block_f = late.take(NG * (NB - 1)), late.take(NG)
        slots_i, part_i = late.take(NC, dt=I32), late.take(NC, dt=I32)
        att_linear = late.take(D)

        l_edges, l_x, l_w, l_w1 = landing("edges"), landing("x"), landing("w"), landing("w1")
        l_vec, l_wide, l_bias = landing("vectors"), landing("wide"), landing("bias")
        edge_view = lambda ap: ap.rearrange("(p j) -> p j", j=EJ)
        l_edges.dma(S, lambda e: e.dma_start(src_in[0:EP, :], edge_view(ins["src"])))
        edges_in = l_edges.dma(S, lambda e: e.dma_start(dst_in[0:EP, :], edge_view(ins["dst"])))
        PAD_FROM = LAST // 32 * 32
        t_pad = G.do(lambda e: e.memset(x_in[PAD_FROM:P, NB - 1, :], 0.0))
        l_x.dma(S, lambda e: e.dma_start(x_in[:, 0:NB - 1, :], ins["x"][0:(NB - 1) * P, :].rearrange("(b p) d -> p b d", p=P)))
        x_loaded = l_x.dma(S, lambda e: e.dma_start(x_in[0:LAST, NB - 1, :], ins["x"][(NB - 1) * P:N, :]), t_pad)
        vectors = {}
        at = 0
        for name, n in (("L0_gnn_ln1_g", KC), ("L0_gnn_ln1_b", KC), ("L0_gnn_ln2_g", KC), ("L0_gnn_ln2_b", KC),
                        ("L1_gnn_ln_g", KC * LAYERS), ("L1_gnn_ln_b", KC * LAYERS), ("L0_gnn_b1", FC)):
            src = ins[name]
            if len(src.shape) == 2:
                src = src.rearrange("l d -> (l d)")
            vectors_in = l_vec.dma(S, lambda e, at=at, n=n, src=src: e.dma_start(columns_in[at:at + n, :], src.rearrange("(k p) -> k p", p=P)))
            vectors[name] = at
            at += n
        assert at == VECTORS
        column = lambda name, k: columns[:, vectors[name] + k:vectors[name] + k + 1]
        spread = lambda ap: ap.unsqueeze(0).broadcast_to([P, ap.shape[0]])
        w_view = lambda ap: ap.rearrange("(k p) n -> p k n", p=P)
        wide_in = l_wide.dma(S, lambda e: e.dma_start(att_linear, spread(ins["L0_gnn_att"].rearrange("h c -> (h c)"))))
        l_w.dma(S, lambda e: e.dma_start(w_left, w_view(ins["L0_gnn_Wl"])))
        w_loaded = l_w.dma(S, lambda e: e.dma_start(w_right, w_view(ins["L0_gnn_Wr"])))
        l_bias.dma(S, lambda e: e.dma_start(gat_bias, spread(ins["L0_gnn_gat_bias"])))
        bias_in = l_bias.dma(S, lambda e: e.dma_start(b2[:, :], spread(ins["L0_gnn_b2"])))
        w1_loaded = l_w1.dma(S, lambda e: e.dma_start(w1, w_view(ins["L0_gnn_W1"])))

        t_digits = G.do(lambda e: e.iota(digits, [[1, HIGH], [0, EJ]], base=0, channel_multiplier=0, allow_small_or_imprecise_dtypes=True), t_pad)
        G.do(lambda e: e.memset(ident[:, :], 0.0))
        g1 = G.do(lambda e: e.memset(ones[:, :], 1.0))
        G.do(lambda e: e.affine_select(out=ident[:, :], in_=ident[:, :], compare_op=ALU.not_equal, fill=1.0,
                                       base=0, pattern=[[-1, P]], channel_multiplier=1), g1)
        G.do(lambda e: e.affine_select(out=earlier[:, :], in_=ones[:, :], compare_op=ALU.is_ge, fill=0.0,
                                       base=-1, pattern=[[1, P]], channel_multiplier=-1), g1)
        G.do(lambda e: e.iota(iota[:, :], [[1, max(NC, EJ)]], base=0, channel_multiplier=0, allow_small_or_imprecise_dtypes=True))
        G.do(lambda e: e.memset(eps[:, :], LN_EPS))
        G.do(lambda e: e.memset(zero[:, :], 0.0))
        t_const = G.do(lambda e: e.iota(iota_node, [[1, NP]], base=0, channel_multiplier=0, allow_small_or_imprecise_dtypes=True))

        t = T.do(lambda e: e.transpose(bank[:, 7, 0:VECTORS], columns_in[0:VECTORS, :], ident[0:VECTORS, 0:VECTORS]), t_const, vectors_in)
        columns_ready = A.do(lambda e: e.activation(columns[:, :], bank[:, 7, 0:VECTORS], ACT.Copy), t)

        R0 = slice(0, EP)

        def ranks(radix, after, shift_for=None):
            m3 = match[R0, 0:radix * EJ].rearrange("p (k j) -> p k j", j=EJ)
            s3 = running[R0, 0:radix * EJ].rearrange("p (k j) -> p k j", j=EJ)
            r3 = ranked[R0, 0:radix * EJ].rearrange("p (k j) -> p k j", j=EJ)
            t = V.do(lambda e: e.tensor_tensor(m3, over(digit[R0, :], 1, radix), digits[R0, 0:radix, :], ALU.is_equal), t_digits, after)
            t = V.do(lambda e: e.tensor_tensor_scan(running[R0, 0:radix * EJ], match[R0, 0:radix * EJ], match[R0, 0:radix * EJ], 0.0, ALU.add, ALU.max), t)
            t1 = V.do(lambda e: e.memset(shifted[R0, 0:1], 0.0))
            t2 = V.do(lambda e: e.tensor_copy(total[R0, 0:radix], s3[:, :, EJ - 1]), t)
            t3 = V.do(lambda e: e.tensor_copy(shifted[R0, 1:radix], s3[:, 0:radix - 1, EJ - 1]))
            t4 = V.do(lambda e: e.tensor_tensor(per_digit[R0, 0:radix], total[R0, 0:radix], shifted[R0, 0:radix], ALU.subtract), t1, t2, t3)
            T.quiet(lambda e: e.matmul(bank[R0, 6, 0:radix], ones[R0, R0], shifted[R0, 0:radix], start=True, stop=False), t_const, t4)
            t5 = T.do(lambda e: e.matmul(bank[R0, 6, 0:radix], earlier[R0, R0], per_digit[R0, 0:radix], start=False, stop=True))
            t6 = V.do(lambda e: e.scalar_tensor_tensor(base_of[R0, 0:radix], bank[R0, 6, 0:radix], -1.0, shifted[R0, 0:radix], ALU.add, ALU.subtract), t5)
            if shift_for is not None:
                t6 = shift_for(t6)
            t7 = V.do(lambda e: e.tensor_tensor(r3, s3, over(base_of[R0, 0:radix], 2, EJ), ALU.add), t6)
            t8 = V.do(lambda e: e.tensor_tensor(r3, r3, m3, ALU.mult), t7)
            return V.do(lambda e: e.tensor_reduce(place[R0, :], r3.rearrange("p k j -> p j k"), AX.X, ALU.add), t8)

        def divide(quotient, value, by, after, remainder=None):
            t = V.do(lambda e: e.tensor_scalar(quotient, value, 1.0 / by, -(by - 1) / 2.0 / by, ALU.mult, ALU.add), after)
            t = V.do(lambda e: e.tensor_scalar(quotient, quotient, ROUND, ROUND, ALU.add, ALU.subtract), t)
            if remainder is None:
                return t
            return V.do(lambda e: e.scalar_tensor_tensor(remainder, quotient, -float(by), value, ALU.mult, ALU.add), t)

        def permute(out_rows, width, row, col, after, b, between=lambda j: None):
            used = [None] * RING
            for j in range(EJ):
                r, c = pick_row[j % RING], pick_col[j % RING]
                V.do(lambda e, j=j, r=r: e.tensor_scalar(r[R0, 0:out_rows], iota[R0, 0:out_rows], row[R0, j:j + 1], None, ALU.is_equal), after, used[j % RING])
                t = V.do(lambda e, j=j, c=c: e.tensor_scalar(c[R0, 0:width], iota[R0, 0:width], col[R0, j:j + 1], packed[R0, j:j + 1], ALU.is_equal, ALU.mult))
                used[j % RING] = T.do(lambda e, j=j, r=r, c=c: e.matmul(bank[0:out_rows, b, 0:width], r[R0, 0:out_rows], c[R0, 0:width], start=(j == 0), stop=(j == EJ - 1)), t)
                between(j)
            return used[(EJ - 1) % RING]

        t1 = V.do(lambda e: e.tensor_copy(src_g[R0, :], src_in[R0, :]), edges_in)
        t2 = V.do(lambda e: e.tensor_copy(dst_g[R0, :], dst_in[R0, :]))
        t3 = V.do(lambda e: e.tensor_scalar(digit_i[R0, :], dst_in[R0, :], LOW - 1, None, ALU.bitwise_and))
        V.do(lambda e: e.scalar_tensor_tensor(packed[R0, :], dst_g[R0, :], float(PACK), src_g[R0, :], ALU.mult, ALU.add), t1, t2)
        t4 = V.do(lambda e: e.tensor_copy(digit[R0, :], digit_i[R0, :]), t3)
        t = ranks(LOW, t4)
        low_ready = divide(place_hi[R0, :], place[R0, :], EJ, t, place_lo[R0, :])

        V.do(lambda e: e.tensor_reduce(is_head[:, :], ident[:, :].rearrange("p (g h) -> p h g", h=HEADS), AX.X, ALU.add), t_const)
        V.do(lambda e: e.tensor_reduce(is_run[:, :], ident[:, :].rearrange("p (g h) -> p g h", h=HEADS), AX.X, ALU.add))
        V.do(lambda e: e.tensor_copy(to_rows[:, :].rearrange("q (g h) -> q g h", h=HEADS), over(ident[0:HEADS, 0:HEADS], 1, SG)))

        norm_turn = [0]
        norm_used = [None] * norm_slots

        def moments_of(rows_ap, *after):
            s = norm_turn[0] % norm_slots
            norm_turn[0] += 1
            t = V.do(lambda e: e.bn_stats(stat[:, s, :], rows_ap), norm_used[s], *after)
            t = V.do(lambda e: e.bn_aggr(moments[:, s, :], stat[:, s, :]), t)
            return s, A.do(lambda e: e.activation(deviation[:, s, :], moments[:, s, 1:2], ACT.Sqrt, bias=eps[:, :]), t)

        def apply_moments(st, out_ap, rows_ap, *after):
            s, t = st
            t = V.do(lambda e: e.reciprocal(rstd[:, s, :], deviation[:, s, :]), t)
            norm_used[s] = V.do(lambda e: e.tensor_scalar(out_ap, rows_ap, moments[:, s, 0:1], rstd[:, s, :], ALU.subtract, ALU.mult), t, *after)
            return norm_used[s]

        def turn(rows_ap, dest, gain, offset, psum, free, *after):
            for k in range(KC):
                t = T.do(lambda e, k=k: e.transpose(bank[:, psum, k * P:(k + 1) * P], rows_ap[:, k * P:(k + 1) * P], ident[:, :]), *after)
            for k in range(KC):
                done = A.do(lambda e, k=k: e.activation(dest[:, k, :], bank[:, psum, k * P:(k + 1) * P], ACT.Identity,
                                                        bias=column(offset[0], offset[1] + k), scale=column(gain[0], gain[1] + k)), t, columns_ready, free)
            return t, done

        t = V.do(lambda e: e.tensor_scalar(att_relu, att_linear, 1.0 - SLOPE, None, ALU.mult), wide_in)
        att_ready = V.do(lambda e: e.tensor_scalar(att_linear, att_linear, SLOPE, None, ALU.mult), t)
        wa_ready = att_ready
        product = ranked[:, 0:KC * D]
        for side, w in ((0, w_left), (1, w_right)):
            p3 = product.rearrange("p (k n) -> p k n", n=D)
            t = V.do(lambda e, w=w: e.tensor_tensor(p3, w, over(att_linear, 1, KC), ALU.mult), w_loaded, wa_ready)
            wa_ready = V.do(lambda e, side=side: e.tensor_reduce(wa[:, side, :, :].rearrange("p k h -> p (k h)"), product.rearrange("p (r c) -> p r c", c=C), AX.X, ALU.add), t)

        twice = [None] * NB
        first = moments_of(x_in[:, 0, :], x_loaded)
        for b in range(NB):
            t = apply_moments(first, x_in[:, b, :], x_in[:, b, :])
            if b + 1 < NB:
                first = moments_of(x_in[:, b + 1, :])
            t = V.do(lambda e, b=b: e.tensor_scalar(state[:, b, :], x_in[:, b, :], 0.0, None, ALU.max), t)
            second = moments_of(state[:, b, :], t)
            if b:
                twice[b - 1] = apply_moments(before, x_in[:, b - 1, :], state[:, b - 1, :])
            before = second
        twice[NB - 1] = apply_moments(before, x_in[:, NB - 1, :], state[:, NB - 1, :])
        for b in range(NB):
            state_ready = G.do(lambda e, b=b: e.tensor_tensor(state[:, b, :], state[:, b, :], gat_bias, ALU.add), twice[b], bias_in)

        tile_free, tables_written = [None] * 4, []
        l_tile = [landing(f"tile{i}") for i in range(4)]

        def projections():
            bank_free, product_read = {}, [None] * 3
            turned_at = [None] * NB
            psum_free = [columns_ready] * 2

            def turn_block(b):
                _, turned_at[b] = turn(x_in[:, b, :], trans[b % 3], ("L0_gnn_ln1_g", 0), ("L0_gnn_ln1_b", 0), b % 2, product_read[b % 3], twice[b], psum_free[b % 2])
                psum_free[b % 2] = turned_at[b]
            turn_block(0)
            yield
            for b in range(NB):
                if b + 1 < NB:
                    turn_block(b + 1)
                    yield
                for side, (w, table) in enumerate(((w_left, left_table), (w_right, right_table))):
                    n = 2 * b + side
                    for k in range(KC):
                        lhs = trans[b % 3][:, k, :]
                        T.quiet(lambda e, k=k, w=w, lhs=lhs, side=side: e.matmul(bank[:, 2 + side, :], lhs, w[:, k, :], start=(k == 0), stop=(k == KC - 1)), turned_at[b], w_loaded, bank_free.get(side))
                        yield
                    for k in range(KC):
                        lhs = trans[b % 3][:, k, :]
                        t = T.do(lambda e, k=k, side=side, lhs=lhs: e.matmul(bank[:, 4 + side, 0:HEADS], lhs, wa[:, side, k, :], start=(k == 0), stop=(k == KC - 1)), wa_ready)
                    product_read[b % 3] = t
                    tl = tile[n % 4]
                    A.do(lambda e, tl=tl, side=side: e.activation(tl[:, 0:D], bank[:, 2 + side, :], ACT.Copy), t, tile_free[n % 4])
                    bank_free[side] = A.do(lambda e, tl=tl, side=side: e.activation(tl[:, D:TW], bank[:, 4 + side, 0:HEADS], ACT.Copy))
                    tile_free[n % 4] = l_tile[n % 4].dma(S, lambda e, tl=tl, table=table, b=b: e.dma_start(table[b * P:(b + 1) * P, :], tl), bank_free[side])
                    tables_written.append(tile_free[n % 4])
                    yield

        projecting = projections()
        STEPS = 1 + NB - 1 + NB * 2 * (KC + 1)

        def project(some):
            for _ in range(some):
                next(projecting, None)

        third = STEPS // 3
        low_sorted = permute(EP, EJ, place_hi, place_lo, low_ready, 6,
                             lambda j: project(1) if (j + 1) * third // EJ > j * third // EJ else None)
        project(third + third // 3)

        t = V.do(lambda e: e.tensor_copy(packed[R0, :], bank[R0, 6, 0:EJ]), low_sorted)
        t1 = V.do(lambda e: e.tensor_copy(digit_i[R0, :], packed[R0, :]), t)
        t1 = V.do(lambda e: e.tensor_scalar(digit_i[R0, :], digit_i[R0, :], (PACK * LOW).bit_length() - 1, None, ALU.arith_shift_right), t1)
        t1 = V.do(lambda e: e.tensor_copy(digit[R0, :], digit_i[R0, :]), t1)
        V.do(lambda e: e.tensor_scalar(packed[R0, :], packed[R0, :], float(PACK), None, ALU.add), t)
        zeroed = []

        def pad_blocks(after):
            t = T.do(lambda e: e.matmul(bank[:, 7, 0:HIGH], ones[R0, :], total[R0, 0:HIGH], start=True, stop=True), after, columns_ready)
            t = V.do(lambda e: e.tensor_copy(block_end, bank[:, 7, 0:HIGH].rearrange("p (b q) -> p b q", q=HPB)[:, :, HPB - 1]), t)
            t1 = V.do(lambda e: e.memset(block_before[:, 0:1], 0.0))
            t2 = V.do(lambda e: e.tensor_copy(block_before[:, 1:NB], block_end[:, 0:NB - 1]), t)
            t = V.do(lambda e: e.tensor_tensor(block_n, block_end, block_before, ALU.subtract), t1, t2)
            t = V.do(lambda e: e.tensor_scalar(block_n, block_n, float(PAIR - 1), None, ALU.add), t)
            t = divide(pairs, block_n, PAIR, t)
            t = V.do(lambda e: e.tensor_tensor_scan(pair_end, pairs, pairs, 0.0, ALU.add, ALU.max), t)
            t = V.do(lambda e: e.tensor_tensor(pair_at, pair_end, pairs, ALU.subtract), t)
            t = V.do(lambda e: e.scalar_tensor_tensor(shift, pair_at, float(PAIR), block_before, ALU.mult, ALU.subtract), t)
            b3 = base_of[R0, 0:HIGH].rearrange("p (b q) -> p b q", q=HPB)
            out_t = V.do(lambda e: e.tensor_tensor(b3, b3, over(shift[R0, :], 2, HPB), ALU.add), t)
            p3 = passed.rearrange("p (g b) -> p g b", b=NB - 1)
            t = V.do(lambda e: e.tensor_tensor(p3, over(pair_at[:, 1:NB], 1, NG), over(iota[:, 0:NG], 2, NB - 1), ALU.is_le), t)
            t = V.do(lambda e: e.tensor_reduce(block_f, p3, AX.X, ALU.add), t)
            zeroed.append(V.do(lambda e: e.tensor_copy(block_of[:, :], block_f[0:1, :]), t))
            return out_t

        t = ranks(HIGH, t1, pad_blocks)
        high_ready = divide(place_hi[R0, :], place[R0, :], P, t, place_lo[R0, :])
        left = STEPS - 2 * third - third // 3
        t = permute(P, NC, place_lo, place_hi, high_ready, 6,
                    lambda j: project(1) if (j + 1) * left // EJ > j * left // EJ else None)
        project(STEPS)
        t = V.do(lambda e: e.tensor_copy(slots_i, bank[:, 6, 0:NC]), t)
        V.do(lambda e: e.tensor_scalar(src_of[:, :], slots_i, PACK - 1, None, ALU.bitwise_and), t)
        t1 = V.do(lambda e: e.tensor_scalar(part_i, slots_i, PACK.bit_length() - 1, None, ALU.arith_shift_right))
        V.do(lambda e: e.tensor_copy(src_f[:, :], src_of[:, :]), t1)
        t = V.do(lambda e: e.tensor_copy(key[:, :], part_i), t1)
        V.do(lambda e: e.tensor_scalar(dst_of[:, :], key[:, :], -1.0, 0.0, ALU.add, ALU.max), t)
        l3 = local[:, :].rearrange("p (g i) -> p g i", i=2)
        t = V.do(lambda e: e.scalar_tensor_tensor(l3, over(block_f, 2, 2), -float(P), key[:, :].rearrange("p (g i) -> p g i", i=2), ALU.mult, ALU.add), t)
        t = V.do(lambda e: e.tensor_scalar(local[:, :], local[:, :], -1.0, None, ALU.add), t)
        slots_ready = V.do(lambda e: e.tensor_scalar(minus_local, local, -1.0, None, ALU.mult), t)
        counts_zero = A.do(lambda e: e.activation(counts[:, :, :], zero[:, 0:1].unsqueeze(2).broadcast_to([P, NB, NP]), ACT.Copy), slots_ready)

        DEPTH = 6
        plan = Plan(0, W1_AT - EARLY)
        gathered = [plan.take(2, TW) for _ in range(DEPTH)]
        weighted = [plan.take(2, D) for _ in range(2)]
        score = plan.take(NC, HEADS)
        hot_at = plan.at
        src_hot = [plan.take(NP, dt=BF16) for _ in range(4)]
        dst_hot = [plan.take(P, dt=BF16) for _ in range(4)]
        src_gap = [plan.take(NP, dt=BF16) for _ in range(2)]
        dst_gap = [plan.take(P, dt=BF16) for _ in range(4)]
        hot_end = plan.at
        minus_src = plan.take(NC)
        weights = plan.take(NC, HEADS + 1)
        hot = [plan.take(P) for _ in range(4)]
        gap = [plan.take(P) for _ in range(4)]
        agg_at = plan.at
        agg = plan.take(NB, D)
        agg_den = plan.take(NB, HEADS + 1)
        agg_end = plan.at

        plan = Plan(agg_at, agg_end)
        turned_key = plan.take(RUN)
        reset = plan.take(RUN)
        key_rows = plan.take(SK, P)
        t = V.do(lambda e: e.memset(weights[:, :, HEADS], 1.0), slots_ready, *tables_written[-4:])
        V.do(lambda e: e.tensor_scalar(minus_src, src_f, -1.0, None, ALU.mult))
        buffers_ready = V.do(lambda e: e.tensor_copy(key_rows.rearrange("p k (g h) -> p k g h", h=HEADS), over(key.rearrange("p (g k) -> p k g", k=SK), 3, HEADS)))
        for k in range(SK):
            keys_turned = T.do(lambda e, k=k: e.transpose(flat[:, k * P:(k + 1) * P], key_rows[:, k, :], ident[:, :]), buffers_ready)

        l_gather = [landing(f"gather{i}") for i in range(DEPTH)]
        l_add = [landing(f"add{i}") for i in range(DEPTH)]
        gather_free = [buffers_ready] * DEPTH
        own = [None] * DEPTH

        def gather(lands, table, index, g, i, add, *after):
            extra = dict(compute_op=ALU.add, bounds_check=NP - 1, oob_is_err=True) if add else {}
            c = 2 * g + i
            return lands.dma(G, lambda e: e.indirect_dma_start(
                out=gathered[g % DEPTH][:, i, :], out_offset=None, in_=table,
                in_offset=bass.IndirectOffsetOnAxis(ap=index[:, c:c + 1], axis=0), **extra), *after)

        def gather_left(g):
            for i in range(2):
                own[g % DEPTH] = gather(l_gather[g % DEPTH], left_table, src_of, g, i, False, gather_free[g % DEPTH], *tables_written[-4:])

        AHEAD = 3
        for g in range(AHEAD):
            gather_left(g)

        t1 = V.do(lambda e: e.tensor_copy(turned_key, flat[:, 0:RUN]), keys_turned)
        V.do(lambda e: e.memset(reset[:, 0:1], 0.0))
        t = V.do(lambda e: e.tensor_tensor(reset[:, 1:RUN], turned_key[:, 1:RUN], turned_key[:, 0:RUN - 1], ALU.not_equal), t1)
        resets_ready = V.do(lambda e: e.tensor_scalar(reset[:, 1:RUN], reset[:, 1:RUN], FAR, None, ALU.mult), t)

        weighted_free, hot_free, src_gap_free, dst_gap_free = [None] * 2, [None] * 4, [None] * 2, [None] * 4
        count_free = [t1, counts_zero]

        def one_hot(out_ap, gap_ap, iota_ap, minus_ap, *after):
            t = A.do(lambda e: e.activation(gap_ap, iota_ap, ACT.Abs, bias=minus_ap), *after)
            return A.do(lambda e: e.activation(out_ap, gap_ap, ACT.Relu, bias=ones[:, 0:1], scale=-1.0), t)

        def count_pair(g):
            lo = 3 * (g % 2)
            for i in range(2):
                c = 2 * g + i
                s = c % 4
                if i == 0:
                    src_t = V.do(lambda e, c=c, s=s: e.tensor_scalar(src_hot[s], iota_node, src_f[:, c:c + 1], None, ALU.is_equal), hot_free[s])
                else:
                    src_t = one_hot(src_hot[s], src_gap[g % 2], iota_node, minus_src[:, c:c + 1], src_gap_free[g % 2], hot_free[s], buffers_ready)
                    src_gap_free[g % 2] = src_t
                dst_t = one_hot(dst_hot[s], dst_gap[s], iota_node[:, 0:P], minus_local[:, c:c + 1], dst_gap_free[s], hot_free[s], buffers_ready)
                dst_gap_free[s] = dst_t
                for b in range(NB):
                    o = flat[:, lo * 512 + b * P:lo * 512 + (b + 1) * P]
                    f = lambda e, s=s, b=b, o=o, i=i: e.matmul(o, src_hot[s][:, b * P:(b + 1) * P], dst_hot[s], start=(i == 0 and b % 4 == 0), stop=(i == 1), skip_group_check=True)
                    if b < NB - 1:
                        T.quiet(f, src_t, dst_t, count_free[g % 2])
                    else:
                        hot_free[s] = T.do(f)
            return hot_free[(2 * g + 1) % 4]

        def block_number(e, g):
            return e.value_load(block_of[0:1, g:g + 1], min_val=0, max_val=NB - 1)

        def add_counts(g, ready):
            lo = 3 * (g % 2)

            def fn(e):
                d = counts[:, :, bass.ds(block_number(e, g) * P, P)]
                return e.tensor_tensor(d, d, flat[:, lo * 512:lo * 512 + NP].rearrange("p (b n) -> p b n", n=P), ALU.add)
            count_free[g % 2] = V.do(fn, ready, counts_zero, count_free[(g + 1) % 2])

        counted = None
        for g in range(NG):
            s = g % DEPTH
            if g + AHEAD < NG:
                gather_left(g + AHEAD)
            for i in range(2):
                t = gather(l_add[s], right_table, dst_of, g, i, True, own[s])
            counting = count_pair(g)
            w = weighted[g % 2]
            t1 = V.do(lambda e, s=s, w=w: e.scalar_tensor_tensor(w, gathered[s][:, :, 0:D], 0.0, over(att_relu, 1, 2), ALU.max, ALU.mult), t, weighted_free[g % 2])
            sc = score[:, 2 * g:2 * g + 2, :]
            t1 = V.do(lambda e, w=w, sc=sc: e.tensor_reduce(sc.rearrange("p i h -> p (i h)"), w.rearrange("p i (h c) -> p (i h) c", c=C), AX.X, ALU.add), t1)
            weighted_free[g % 2] = t1
            gather_free[s] = V.do(lambda e, s=s, sc=sc: e.tensor_tensor(sc, sc, gathered[s][:, :, D:TW], ALU.add), t1)
            if g:
                add_counts(g - 1, counted)
            counted = counting
        add_counts(NG - 1, counted)
        scores_ready = gather_free[(NG - 1) % DEPTH]

        l_again = [landing(f"again{i}") for i in range(DEPTH)]
        landed = [None] * DEPTH

        def gather_again(g):
            for i in range(2):
                landed[g % DEPTH] = gather(l_again[g % DEPTH], left_table, src_of, g, i, False, gather_free[g % DEPTH])
        for g in range(DEPTH - 1):
            gather_again(g)

        plan = Plan(hot_at, hot_end)
        behind_max = plan.take(RUN)
        turned = plan.take(RUN)
        plan = Plan(agg_at + 2 * RUN, agg_end)
        ahead_max = plan.take(RUN)
        ends = plan.take(4 * SG)
        small = plan.take(10 * SG)
        carry_rows = plan.take(2 * SG)
        carry = plan.take(2)
        score_rows = Plan(DEPTH * 2 * TW).take(SK, P)
        t2 = V.do(lambda e: e.tensor_copy(score_rows.rearrange("p k (g h) -> p k g h", h=HEADS), score.rearrange("p (g k) h -> p k g h", k=SK)), scores_ready)
        for k in range(SK):
            ts = T.do(lambda e, k=k: e.transpose(flat[:, k * P:(k + 1) * P], score_rows[:, k, :], ident[:, :]), t2, count_free[0], count_free[1])
        t2 = V.do(lambda e: e.tensor_copy(turned, flat[:, 0:RUN]), ts)
        t5 = V.do(lambda e: e.tensor_tensor_scan(ahead_max, reset, turned, FAR, ALU.add, ALU.max), t2, resets_ready)
        t6 = V.do(lambda e: e.tensor_copy(behind_max[:, RUN - 1:RUN], turned[:, RUN - 1:RUN]))
        t7 = V.do(lambda e: e.tensor_tensor_scan(behind_max[:, 0:RUN - 1][:, ::-1], reset[:, 1:RUN][:, ::-1], turned[:, 0:RUN - 1][:, ::-1],
                                                 turned[:, RUN - 1:RUN], ALU.add, ALU.max), t6)
        for n, col in enumerate((ahead_max[:, RUN - 1:RUN], behind_max[:, 0:1], turned_key[:, 0:1], turned_key[:, RUN - 1:RUN])):
            t = V.do(lambda e, n=n, col=col: e.tensor_scalar(ends[:, n * SG:(n + 1) * SG], is_run[:, :], col, None, ALU.mult), t5, t7)
        t = T.do(lambda e: e.matmul(bank[0:HEADS, 6, 0:4 * SG], is_head[:, :], ends, start=True, stop=True), t)
        H8 = slice(0, HEADS)
        right_end, left_end, first_key, last_key, wall, wall_b, over_f, over_b, chain_f, chain_b = [small[H8, i * SG:(i + 1) * SG] for i in range(10)]
        t = V.do(lambda e: e.tensor_copy(small[H8, 0:4 * SG], bank[0:HEADS, 6, 0:4 * SG]), t)
        carry_f, carry_b = carry_rows[H8, 0:SG], carry_rows[H8, SG:2 * SG]

        def walls(dest, one, other, *after):
            t = V.do(lambda e: e.tensor_tensor(dest, one, other, ALU.not_equal), *after)
            return V.do(lambda e: e.tensor_scalar(dest, dest, FAR, None, ALU.mult), t)
        V.do(lambda e: e.memset(small[H8, 4 * SG:8 * SG], 0.0))
        t0 = V.do(lambda e: e.memset(carry_rows[H8, :], FAR))
        ta = walls(wall[:, 1:SG], last_key[:, 1:SG], last_key[:, 0:SG - 1], t, t0)
        tb = walls(wall_b[:, 0:SG - 1], first_key[:, 0:SG - 1], first_key[:, 1:SG])
        tc = walls(over_f[:, 1:SG], first_key[:, 1:SG], last_key[:, 0:SG - 1])
        ta = V.do(lambda e: e.tensor_tensor_scan(chain_f, wall, right_end, FAR, ALU.add, ALU.max), ta)
        tb = V.do(lambda e: e.tensor_tensor_scan(chain_b[:, ::-1], wall_b[:, ::-1], left_end[:, ::-1], FAR, ALU.add, ALU.max), tb)
        V.do(lambda e: e.tensor_tensor(carry_f[:, 1:SG], chain_f[:, 0:SG - 1], over_f[:, 1:SG], ALU.add), ta, tc)
        t = V.do(lambda e: e.tensor_tensor(carry_b[:, 0:SG - 1], chain_b[:, 1:SG], over_f[:, 1:SG], ALU.add), tb)
        t = T.do(lambda e: e.matmul(bank[:, 6, 128:128 + 2 * SG], to_rows[:, :], carry_rows[H8, :], start=True, stop=True), t)
        c3 = ends[:, 0:2 * SG].rearrange("p (w g) -> p w g", w=2)
        t = V.do(lambda e: e.tensor_tensor(c3, bank[:, 6, 128:128 + 2 * SG].rearrange("p (w g) -> p w g", w=2), over(is_run[:, :], 1, 2), ALU.mult), t)
        t = V.do(lambda e: e.tensor_reduce(carry, c3, AX.X, ALU.add), t)
        t1 = V.do(lambda e: e.tensor_scalar(reset, turned_key, turned_key[:, 0:1], FAR, ALU.not_equal, ALU.mult), t5)
        m1 = V.do(lambda e: e.scalar_tensor_tensor(ahead_max, reset, carry[:, 0:1], ahead_max, ALU.add, ALU.max), t, t1)
        t1 = V.do(lambda e: e.tensor_scalar(reset, turned_key, turned_key[:, RUN - 1:RUN], FAR, ALU.not_equal, ALU.mult), m1)
        m2 = V.do(lambda e: e.scalar_tensor_tensor(behind_max, reset, carry[:, 1:2], behind_max, ALU.add, ALU.max), t1)
        t = V.do(lambda e: e.tensor_tensor(ahead_max, ahead_max, behind_max, ALU.max), m2)
        max_ready = V.do(lambda e: e.tensor_tensor(turned, turned, ahead_max, ALU.subtract), t)
        t = A.do(lambda e: e.activation(turned, turned, ACT.Exp), max_ready)
        for k in range(SK):
            tw = T.do(lambda e, k=k: e.transpose(flat[:, k * P:(k + 1) * P], turned[:, k * P:(k + 1) * P], ident[:, :]), t)
        G.do(lambda e: e.memset(agg, 0.0), max_ready)
        agg_zero = G.do(lambda e: e.memset(agg_den, 0.0))
        w4 = weights[:, :, 0:HEADS].rearrange("p (g k) h -> p k g h", k=SK)
        weights_ready = V.do(lambda e: e.tensor_copy(w4, flat[:, 0:RUN].rearrange("p (k g h) -> p k g h", g=SG, h=HEADS)), tw)

        hot_free, gap_free = [None] * 4, [None] * 4
        weighted_free = [weights_ready] * 2
        sum_free = [agg_zero] * 2

        def add_sums(g, ready):
            b0 = g % 2

            def both(e):
                r = block_number(e, g)
                d = agg[:, bass.ds(r, 1), :].rearrange("p b n -> p (b n)")
                e.tensor_tensor(d, d, bank[:, b0, :], ALU.add).then_inc(V.sem, 1)
                d = agg_den[:, bass.ds(r, 1), :].rearrange("p b n -> p (b n)")
                return e.tensor_tensor(d, d, bank[:, 2 + b0, 0:HEADS + 1], ALU.add)
            V.count += 1
            sum_free[g % 2] = V.do(both, ready, sum_free[(g + 1) % 2])

        pending = None
        for g in range(NG):
            s = g % DEPTH
            w = weighted[g % 2]
            msg_t = V.do(lambda e, s=s, w=w, g=g: e.tensor_tensor(
                w.rearrange("p i (h c) -> p i h c", c=C), gathered[s][:, :, 0:D].rearrange("p i (h c) -> p i h c", c=C),
                over(weights[:, 2 * g:2 * g + 2, 0:HEADS], 3, C), ALU.mult), landed[s], weighted_free[g % 2])
            gather_free[s] = msg_t
            if g + DEPTH - 1 < NG:
                gather_again(g + DEPTH - 1)
            for i in range(2):
                c = 2 * g + i
                h = hot[c % 4]
                hot_t = one_hot(h, gap[c % 4], iota[:, 0:P], minus_local[:, c:c + 1], gap_free[c % 4], hot_free[c % 4])
                gap_free[c % 4] = hot_t
                T.quiet(lambda e, h=h, w=w, i=i, g=g: e.matmul(bank[:, g % 2, :], h, w[:, i, :], start=(i == 0), stop=(i == 1)), msg_t, hot_t, sum_free[g % 2])
                hot_free[c % 4] = T.do(lambda e, h=h, c=c, i=i, g=g: e.matmul(bank[:, 2 + g % 2, 0:HEADS + 1], h, weights[:, c, :], start=(i == 0), stop=(i == 1)))
            weighted_free[g % 2] = hot_free[(2 * g + 1) % 4]
            if pending:
                add_sums(*pending)
            pending = (g, hot_free[(2 * g + 1) % 4])
        add_sums(*pending)
        sums_done = sum_free[(NG - 1) % 2]

        w2 = Plan(0).take(FC, D)
        plan = Plan(FC * D, W1_AT)
        trans2 = plan.take(KC, NP)
        hidden = plan.take(FC, GROUP * P)
        assert plan.at <= W1_AT - 4 * D and agg_end <= W1_AT - 4 * D
        plan = Plan(W1_AT - 4 * D, W1_AT)
        rows2 = [plan.take(D) for _ in range(2)]
        x_again = [plan.take(D) for _ in range(2)]
        assert FC * D + KC * NP <= agg_at
        l_w2 = landing("w2")
        w2_loaded = l_w2.dma(S, lambda e: e.dma_start(w2, w_view(ins["L0_gnn_W2"])), weighted_free[(NG - 1) % 2], sums_done)
        in_degree = V.do(lambda e: e.tensor_scalar(norm_dst[:, :], agg_den[:, :, HEADS], 1.0, None, ALU.max), sums_done)
        t = V.do(lambda e: e.tensor_scalar(agg_den, agg_den, 1e-16, None, ALU.add), in_degree)
        den_ready = V.do(lambda e: e.reciprocal(agg_den, agg_den), t)
        normed, turned_b = [None] * NB, [None] * NB
        rows_read = [None] * 2
        turn_free = [weights_ready] * 2

        def add_attention(b):
            a3 = agg[:, b, :].rearrange("p (h c) -> p h c", c=C)
            t = V.do(lambda e: e.tensor_tensor(a3, a3, over(agg_den[:, b, 0:HEADS], 2, C), ALU.mult), den_ready)
            return V.do(lambda e: e.tensor_tensor(state[:, b, :], state[:, b, :], agg[:, b, :], ALU.add), t, state_ready)

        def turn_rows(b):
            rows_read[b % 2], turned_b[b] = turn(rows2[b % 2], trans2[:, :, b * P:(b + 1) * P], ("L0_gnn_ln2_g", 0), ("L0_gnn_ln2_b", 0), 6 + b % 2, turn_free[b % 2], normed[b])
            turn_free[b % 2] = turned_b[b]

        ahead = moments_of(state[:, 0, :], add_attention(0))
        for b in range(GROUP):
            st, ahead = ahead, moments_of(state[:, b + 1, :], add_attention(b + 1))
            normed[b] = apply_moments(st, rows2[b % 2], state[:, b, :], rows_read[b % 2], sums_done)
            turn_rows(b)
        x1_ready = {b: add_attention(b) for b in range(GROUP + 1, NB)}
        agg_read = x1_ready[NB - 1]

        def rows_behind():
            st = ahead
            for b in range(GROUP, NB):
                t = moments_of(state[:, b + 1, :], x1_ready[b + 1]) if b + 1 < NB else None
                normed[b] = apply_moments(st, rows2[b % 2], state[:, b, :], rows_read[b % 2])
                turn_rows(b)
                st = t
                yield
        behind = rows_behind()

        hid_free, out_free, rest_ready, x2_moments = [None] * 2, [None] * GROUP, [None] * NB, [None] * NB

        def residuals():
            l_x2 = [landing("x_again0"), landing("x_again1")]
            again_free = [agg_read] * 2
            for b in range(NB):
                n = min(P, N - b * P)
                G.do(lambda e, b=b: e.tensor_tensor(state[:, b, :], state[:, b, :], b2[:, :], ALU.add), normed[b])
                t = (G.sem, G.count)
                again = l_x2[b % 2].dma(S, lambda e, b=b, n=n: e.dma_start(x_again[b % 2][0:n, :], ins["x"][b * P:b * P + n, :]), again_free[b % 2])
                again_free[b % 2] = rest_ready[b] = G.do(lambda e, b=b, n=n: e.tensor_tensor(state[0:n, b, :], state[0:n, b, :], x_again[b % 2][0:n, :], ALU.add), again, t)

        def degrees():
            t = V.do(lambda e: e.tensor_reduce(norm_src[:, :], counts[:, :, :], AX.X, ALU.add), count_free[0], count_free[1])
            t1 = V.do(lambda e: e.tensor_scalar(norm_src[:, :], norm_src[:, :], 1.0, None, ALU.max), t)
            A.do(lambda e: e.activation(norm_src[:, :], norm_src[:, :], ACT.Sqrt), t1)
            t = A.do(lambda e: e.activation(norm_dst[:, :], norm_dst[:, :], ACT.Sqrt), in_degree)
            V.do(lambda e: e.reciprocal(norm_src[:, :], norm_src[:, :]), t)
            t = V.do(lambda e: e.reciprocal(norm_dst[:, :], norm_dst[:, :]))
            return t, V.do(lambda e: e.tensor_reduce(most[:, :], counts[:, :, :].rearrange("p b n -> p (b n)"), AX.X, ALU.max))

        for g0 in range(0, NB, GROUP):
            blocks = range(g0, min(NB, g0 + GROUP))
            cols = min(len(blocks) * P, N - g0 * P)
            for f in range(FC):
                for k in range(KC):
                    t = T.do(lambda e, f=f, k=k, g0=g0, cols=cols: e.matmul(bank[:, f % 2, 0:cols], w1[:, k, f * P:(f + 1) * P], trans2[:, k, g0 * P:g0 * P + cols], start=(k == 0), stop=(k == KC - 1)),
                             w1_loaded, turned_b[blocks[-1]], hid_free[f % 2])
                hid_free[f % 2] = A.do(lambda e, f=f, cols=cols: e.activation(hidden[:, f, 0:cols], bank[:, f % 2, 0:cols], ACT.Gelu, bias=column("L0_gnn_b1", f)), t, agg_read)
                if g0 == 0 and f % 2:
                    next(behind, None)
            if g0 == 0:
                residuals()
                norms_ready, most_ready = degrees()
            if g0 + GROUP >= NB:
                w1_read = t
            for q, b in enumerate(blocks):
                n = min(P, N - b * P)
                for f in range(FC):
                    t = T.do(lambda e, f=f, q=q, n=n: e.matmul(bank[0:n, 2 + q, :], hidden[:, f, q * P:q * P + n], w2[:, f, :], start=(f == 0), stop=(f == FC - 1)),
                             hid_free[(FC - 1) % 2], w2_loaded, out_free[q])
                out_free[q] = V.do(lambda e, b=b, q=q, n=n: e.tensor_tensor(state[0:n, b, :], state[0:n, b, :], bank[0:n, 2 + q, :], ALU.add), t, rest_ready[b])
                x2_moments[b] = moments_of(state[:, b, :], out_free[q])

            if g0 == 0:
                t = T.do(lambda e: e.transpose(bank[0:1, 7, 0:P], most[:, :], ident[:, :]), most_ready, turned_b[NB - 1])
                t = V.do(lambda e: e.tensor_reduce(most_row[:, :], bank[0:1, 7, 0:P], AX.X, ALU.max), t)
                flag_ready = V.do(lambda e: e.tensor_scalar(exact_flag[:, :], most_row[:, :], EXACT, None, ALU.is_le), t)

        plan = Plan(W1_AT)
        w_raw = plan.take(KC, D)
        w_hi, w_lo = plan.rounded("w_hi", KC, D), plan.rounded("w_lo", KC, D)
        layer_bias = plan.take(LAYERS, D)
        plan = Plan(0, W1_AT)
        hw_hi = [plan.rounded(f"hw_hi{i}", NB, D) for i in range(2)]
        hw_lo = [plan.rounded(f"hw_lo{i}", NB, D) for i in range(2)]
        trans_hi = [plan.rounded(f"trans_hi{i}", KC, P) for i in range(2)]
        trans_lo = [plan.rounded(f"trans_lo{i}", KC, P) for i in range(2)]
        assert plan.at <= W1_AT - 5 * D
        plan = Plan(W1_AT - 5 * D, W1_AT)
        h = [plan.take(D) for _ in range(2)]
        rows3 = [plan.take(D) for _ in range(2)]
        trans3 = plan.take(KC, P)
        split = lambda ap: ap.bitcast(F32)
        in_float32r = [True]

        l_lw, l_lb, l_out = landing("layer_w"), landing("layer_bias"), landing("out")
        split_done, w_split = w1_read, {}

        def load_w(i):
            return l_lw.dma(S, lambda e: e.dma_start(w_raw, w_view(ins["L1_gnn_W"][i, :, :])), split_done)

        def split_w(loaded, read):
            t = G.do(lambda e: e.tensor_copy(w_hi, w_raw), loaded, read)
            return V.do(lambda e: e.tensor_tensor(w_lo, w_raw, split(w_hi), ALU.subtract), t, read)
        lw = load_w(0)
        for i in range(LAYERS):
            bias_loaded = l_lb.dma(S, lambda e, i=i: e.dma_start(layer_bias[:, i, :], spread(ins["L1_gnn_b"][i, :])), w1_read)
        split_done = split_w(lw, w1_read)
        rows_read, rows_done = [None] * 2, [None] * 2
        turned_t, turn_free, trans3_free, trans_read = [None] * 2, [None] * 2, None, [None] * 2
        mul_free, agg_free = [None] * 2, [None] * 2
        hw_ready = {}

        def rows_of(b, *after):
            st = moments_of(h[b % 2], *after)
            rows_done[b % 2] = apply_moments(st, rows3[b % 2], h[b % 2], rows_read[b % 2])

        def turn_of(i, b):
            nonlocal trans3_free
            s = b % 2
            rows_read[s], t = turn(rows3[s], trans3, ("L1_gnn_ln_g", i * KC), ("L1_gnn_ln_b", i * KC), s, turn_free[s], trans3_free, rows_done[s])
            turn_free[s] = t
            t = G.do(lambda e: e.tensor_copy(trans_hi[s], trans3), t, trans_read[s])
            turned_t[s] = trans3_free = V.do(lambda e: e.tensor_tensor(trans_lo[s], trans3, split(trans_hi[s]), ALU.subtract), t)

        def project_of(i, b):
            s = b % 2
            terms = [(lhs, rhs, k) for lhs, rhs in ((trans_hi[s], w_hi), (trans_hi[s], w_lo), (trans_lo[s], w_hi)) for k in range(KC)]
            for n, (lhs, rhs, k) in enumerate(terms):
                t = T.do(lambda e, lhs=lhs, rhs=rhs, k=k, n=n: e.matmul(bank[:, 2 + s, :], lhs[:, k, :], rhs[:, k, :], start=(n == 0), stop=(n == len(terms) - 1)),
                         turned_t[s], split_done, mul_free[s])
            trans_read[s] = t
            t = A.do(lambda e: e.activation(hw_hi[i % 2][:, b, :], bank[:, 2 + s, :], ACT.Copy, scale=norm_src[:, b:b + 1]), t, norms_ready)
            mul_free[s] = hw_ready[i, b] = V.do(lambda e: e.scalar_tensor_tensor(hw_lo[i % 2][:, b, :], bank[:, 2 + s, :], norm_src[:, b:b + 1], split(hw_hi[i % 2][:, b, :]), ALU.mult, ALU.subtract), t)

        def aggregate(i, b, sources):
            n = min(P, N - b * P)
            for s in sources:
                for part in (hw_hi, hw_lo):
                    def product(e, s=s, part=part):
                        lhs, rhs = counts_r[:, s, b * P:b * P + n], part[i % 2][:, s, :]
                        if not in_float32r[0]:
                            lhs, rhs = counts[:, s, b * P:b * P + n], split(rhs)
                        return e.matmul(bank[0:n, 4 + b % 2, :], lhs, rhs, start=(s == 0 and part is hw_hi), stop=(s == NB - 1 and part is hw_lo))
                    t = T.do(product,
                             hw_ready[i, s], counts_rounded, agg_free[b % 2])
            return t

        def finish(i, b, t):
            n = min(P, N - b * P)
            s = b % 2
            agg_free[s] = t = V.do(lambda e: e.scalar_tensor_tensor(h[s][0:n, :], bank[0:n, 4 + s, :], norm_dst[0:n, b:b + 1], layer_bias[0:n, i, :], ALU.mult, ALU.add), t, rows_done[s], bias_loaded)
            if i < LAYERS - 1:
                t = V.do(lambda e: e.tensor_scalar(h[s][0:n, :], h[s][0:n, :], 0.0, None, ALU.max), t)
                rows_of(b, t)
            else:
                t = V.do(lambda e: e.tensor_tensor(state[0:n, b, :], h[s][0:n, :], state[0:n, b, :], ALU.add), t)
                rows_done[s] = t
                l_out.dma(S, lambda e: e.dma_start(out[b * P:b * P + n, :], state[0:n, b, :]), t)

        def by_flag(e, exact, otherwise):
            e.cond(e.value_load(exact_flag[0:1, 0:1], min_val=0, max_val=1), exact, otherwise)

        V.wait(norms_ready, most_ready, flag_ready)
        V.count += 1
        V.ops.append(lambda e: by_flag(e, lambda: e.tensor_copy(counts_r[:, :, :], counts[:, :, :]).then_inc(V.sem, 1),
                                       lambda: e.tensor_copy(most[:, :], zero[:, :]).then_inc(V.sem, 1)))
        counts_rounded = (V.sem, V.count)
        T.wait(flag_ready)
        before = len(T.ops)

        for b in range(NB):
            t = apply_moments(x2_moments[b], h[b % 2], state[:, b, :], rows_done[b % 2])
            t = V.do(lambda e, b=b: e.tensor_scalar(h[b % 2], h[b % 2], 0.0, None, ALU.max), t)
            rows_of(b, t)
            turn_of(0, b)
            if b:
                project_of(0, b - 1)
        pending = [lambda: project_of(0, NB - 1)]
        for i in range(LAYERS):
            for b in range(NB):
                cuts = [0, NB - 1, NB] if i == 0 and b == 0 else [0, NB - 3, NB - 1, NB] if b == 0 else [0, NB]
                for at in range(len(cuts) - 1):
                    t = aggregate(i, b, range(cuts[at], cuts[at + 1]))
                    if pending and at < len(cuts) - 2:
                        pending.pop(0)()
                if b == 0 and i < LAYERS - 1:
                    read = (T.sem, T.count)
                    lw = load_w(i + 1)
                    split_done = split_w(lw, read)
                finish(i, b, t)
                if i < LAYERS - 1:
                    if b >= 1:
                        turn_of(i + 1, b - 1)
                    if b >= 2:
                        project_of(i + 1, b - 2)
            if i < LAYERS - 1:
                def last_rows(i=i):
                    turn_of(i + 1, NB - 1)
                    project_of(i + 1, NB - 2)
                pending = [last_rows, lambda i=i: project_of(i + 1, NB - 1)]

        convolutions = T.ops[before:]
        del T.ops[before:]

        def lay_down(e, exact):
            in_float32r[0] = exact
            for op in convolutions:
                op(e)
        T.ops.append(lambda e: by_flag(e, lambda: lay_down(e, True), lambda: lay_down(e, False)))

        for l in landings:
            S.wait((l.sem, l.count))
        with nc.Block() as block:
            block.vector(V.run)
            block.scalar(A.run)
            block.tensor(T.run)
            block.gpsimd(G.run)
            block.sync(S.run)


_INS = ['x', 'src', 'dst', 'L0_gnn_ln1_g', 'L0_gnn_ln1_b', 'L0_gnn_Wl', 'L0_gnn_Wr', 'L0_gnn_att', 'L0_gnn_gat_bias',
        'L0_gnn_ln2_g', 'L0_gnn_ln2_b', 'L0_gnn_W1', 'L0_gnn_b1', 'L0_gnn_W2', 'L0_gnn_b2', 'L1_gnn_ln_g', 'L1_gnn_ln_b',
        'L1_gnn_W', 'L1_gnn_b']


def kernel(**inputs):
    import numpy as _np
    import concourse.bacc as _bacc
    from concourse import mybir as _mybir
    from concourse.bass_utils import run_bass_kernel_spmd as _run

    nc = _bacc.Bacc("TRN2", target_bir_lowering=False, num_devices=1)
    arrays, args = {}, {}
    for name in _INS:
        a = _np.ascontiguousarray(inputs[name])
        arrays[f"in_{name}_dram"] = a
        args[name] = nc.dram_tensor(f"in_{name}_dram", a.shape, _mybir.dt.from_np(a.dtype), kind="ExternalInput").ap()
    out = nc.dram_tensor("out_0_dram", args["x"].shape, _mybir.dt.float32, kind="ExternalOutput").ap()
    build(nc, args, out)
    r = _run(nc, [arrays], core_ids=[0])
    return r.results[0]["out_0_dram"]
```

```python
from contextlib import ExitStack

import concourse.bass as bass
from concourse import mybir

ALU = mybir.AluOpType
ACT = mybir.ActivationFunctionType
AX = mybir.AxisListType
F32 = mybir.dt.float32
BF16 = mybir.dt.bfloat16
FP16 = mybir.dt.float16
I32 = mybir.dt.int32
F32R = mybir.dt.float32r

P = 128
ROUND = 1.5 * 2.0 ** 23
EXACT = 4096.0
FAR = -1.0e30
LN_EPS = 1e-5
SLOPE = 0.2


class Queue:

    def __init__(self, sem):
        self.sem, self.count, self.ops, self.seen = sem, 0, [], {}

    def wait(self, *after):
        for token in after:
            if token is None:
                continue
            sem, value = token
            if self.seen.get(id(sem), 0) < value:
                self.seen[id(sem)] = value
                self.ops.append(lambda e, sem=sem, value=value: e.wait_ge(sem, value))

    def do(self, fn, *after):
        self.wait(*after)
        self.count += 1
        self.ops.append(lambda e: fn(e).then_inc(self.sem, 1))
        return (self.sem, self.count)

    def quiet(self, fn, *after):
        self.wait(*after)
        self.ops.append(fn)

    def run(self, engine):
        for op in self.ops:
            op(engine)


class Landing:

    def __init__(self, sem):
        self.sem, self.count = sem, 0

    def dma(self, queue, fn, *after):
        queue.wait(*after)
        self.count += 16
        queue.ops.append(lambda e: fn(e).then_inc(self.sem, 16))
        return (self.sem, self.count)


def build(nc, ins, out):
    N, D = ins["x"].shape
    E = ins["src"].shape[0]
    HEADS, C = ins["L0_gnn_att"].shape
    F = ins["L0_gnn_W1"].shape[1]
    LAYERS = ins["L1_gnn_W"].shape[0]
    NB = -(-N // P)
    NP = NB * P
    LAST = N - (NB - 1) * P
    KC = D // P
    FC = F // P
    EP = 125
    EJ = E // EP
    LOW = 32
    HIGH = NP // LOW
    HPB = P // LOW
    PACK = 2048
    PAIR = 2 * P
    NG = (E + NB * (PAIR - 1)) // PAIR
    NC = 2 * NG
    TW = D + HEADS
    SG = P // HEADS
    SK = NC // SG
    RUN = SK * P
    GROUP = 4
    VECTORS = KC * (4 + 2 * LAYERS) + FC
    assert E == EP * EJ and N < PACK and SG * SK == NC and NP % LOW == 0

    with ExitStack() as ctx:
        sem = lambda n: ctx.enter_context(nc.semaphore(n))
        V, A, T, G, S = [Queue(sem("s_" + n)) for n in ("vector", "scalar", "tensor", "gpsimd", "sync")]
        landings = []

        def landing(name):
            landings.append(Landing(sem("d_" + name)))
            return landings[-1]

        def sb(name, shape, dt=F32):
            return ctx.enter_context(nc.sbuf_tensor(name, shape, dt))

        left_table = nc.dram_tensor("left_table", (NP, TW), F32, kind="Internal").ap()
        right_table = nc.dram_tensor("right_table", (NP, TW), F32, kind="Internal").ap()

        bank = ctx.enter_context(nc.psum_tensor("bank", [P, 8, 512], F32))
        flat = bank[:, :, :].rearrange("p b n -> p (b n)")

        ident = sb("ident", [P, P])
        ones = sb("ones", [P, P])
        iota = sb("iota", [P, max(NC, EJ)])
        is_head = sb("is_head", [P, HEADS])
        is_run = sb("is_run", [P, SG])
        to_rows = sb("to_rows", [HEADS, P])
        columns = sb("columns", [P, VECTORS])
        b2 = sb("b2", [P, D])
        eps = sb("eps", [P, 1])
        zero = sb("zero", [P, 1])
        state = sb("state", [P, NB, D])
        block_of = sb("block_of", [1, NG], I32)
        exact_flag = sb("exact_flag", [1, 1], I32)
        most = sb("most", [P, NB])
        most_row = sb("most_row", [NB, 1])
        most_of_all = sb("most_of_all", [1, 1])
        norm_slots = NB + 2
        stat = sb("stat", [P, norm_slots, 6])
        moments = sb("moments", [P, norm_slots, 2])
        deviation = sb("deviation", [P, norm_slots, 1])
        rstd = sb("rstd", [P, norm_slots, 1])
        x2_scale = sb("x2_scale", [P, NB])
        x2_shift = sb("x2_shift", [P, NB])
        norm_src = sb("norm_src", [P, NB])
        norm_dst = sb("norm_dst", [P, NB])
        aligned = lambda at: -(-at // 32) * 32
        counts_at = aligned(nc.sbuf_base)
        counts = sb("counts", [P, NB, NP])
        counts_r = nc.alloc_sbuf_tensor_at("counts_r", [P, NB, NP], F32R, offset=counts_at)
        arena_at = aligned(nc.sbuf_base)
        SIZE = (nc.sbuf_usable_end - arena_at) // 32 * 8
        arena = sb("arena", [P, SIZE])

        class Plan:

            def __init__(self, at, end=SIZE, base=arena):
                self.at, self.end, self.base = at, end, base

            def room(self, words):
                assert self.at + words <= self.end, (self.at, words, self.end)
                self.at += words
                return self.at - words

            def take(self, *shape, dt=F32):
                size = 1
                for n in shape:
                    size *= n
                words = size if dt in (F32, I32) else -(-size // 2)
                at = self.room(words)
                ap = self.base[:, at:at + words]
                if dt is not F32:
                    ap = ap.bitcast(dt)
                if len(shape) > 1:
                    names = " ".join(f"a{i}" for i in range(len(shape)))
                    ap = ap.rearrange(f"p ({names}) -> p {names}", **{f"a{i}": n for i, n in enumerate(shape)})
                return ap

            def rounded(self, name, *shape):
                size = 1
                for n in shape:
                    size *= n
                at = self.room(size)
                t = nc.alloc_sbuf_tensor_at(name, [P, *shape], F32R, offset=arena_at + 4 * at)
                return t[(slice(None),) * (1 + len(shape))]

        def over(ap, axis, n):
            shape = list(ap.shape)
            shape.insert(axis, n)
            return ap.unsqueeze(axis).broadcast_to(shape)

        W1_AT = SIZE - KC * F
        w1 = Plan(W1_AT).take(KC, F)
        EARLY = aligned(4 * (NP // 2 + D + P + 6 * NC + D)) // 4
        plan = Plan(W1_AT - EARLY, W1_AT)
        iota_node = plan.take(NP, dt=FP16)
        gat_bias = plan.take(D)
        earlier = plan.take(P)
        src_of, dst_of = plan.take(NC, dt=I32), plan.take(NC, dt=I32)
        src_f = plan.take(NC)
        key = plan.take(NC)
        local = plan.take(NC)
        minus_local = plan.take(NC)
        att_relu = plan.take(D)

        plan = Plan(0, W1_AT - EARLY)
        x_in = plan.take(NB, D)
        trans = [plan.take(KC, P) for _ in range(3)]
        w_left = plan.take(KC, D)
        w_right = plan.take(KC, D)
        wa = plan.take(2, KC, HEADS)
        tile = [plan.take(TW) for _ in range(4)]
        scratch = plan.take(KC * D)
        ranked = plan.take(HIGH * EJ)
        sort = Plan(0, NB * NP, counts[:, :, :].rearrange("p b n -> p (b n)"))
        digit = sort.take(EJ, dt=BF16)
        digits = sort.take(HIGH, EJ, dt=BF16)
        match = sort.take(HIGH * EJ, dt=BF16)
        running = sort.take(HIGH * EJ, dt=BF16)
        EARLY_ZEROS = sort.at // NP
        src_in, dst_in, digit_i = sort.take(EJ, dt=I32), sort.take(EJ, dt=I32), sort.take(EJ, dt=I32)
        src_g, dst_g, packed, place, place_hi, place_lo, minus_row = [sort.take(EJ) for _ in range(7)]
        total, shifted, per_digit, base_of = [sort.take(HIGH) for _ in range(4)]
        block_end, block_before, block_n, pairs, pair_end, pair_at, shift = [sort.take(NB) for _ in range(7)]
        columns_in = sort.take(P)
        RING = 8
        rings = Plan(0, HIGH * EJ, ranked)
        pick_row = [rings.take(P) for _ in range(RING)]
        pick_col = [rings.take(max(NC, EJ)) for _ in range(RING)]
        pick_gap = [rings.take(P) for _ in range(RING)]
        late = Plan(0, KC * D, scratch)
        passed, block_f = late.take(NG * (NB - 1)), late.take(NG)
        slots_i, part_i = late.take(NC, dt=I32), late.take(NC, dt=I32)
        att_linear = late.take(D)

        l_edges, l_x, l_w, l_w1 = landing("edges"), landing("x"), landing("w"), landing("w1")
        l_vec, l_wide, l_bias = landing("vectors"), landing("wide"), landing("bias")
        edge_view = lambda ap: ap.rearrange("(p j) -> p j", j=EJ)
        l_edges.dma(S, lambda e: e.dma_start(src_in[0:EP, :], edge_view(ins["src"])))
        edges_in = l_edges.dma(S, lambda e: e.dma_start(dst_in[0:EP, :], edge_view(ins["dst"])))
        PAD_FROM = LAST // 32 * 32
        t_pad = G.do(lambda e: e.memset(x_in[PAD_FROM:P, NB - 1, :], 0.0))
        l_x.dma(S, lambda e: e.dma_start(x_in[:, 0:NB - 1, :], ins["x"][0:(NB - 1) * P, :].rearrange("(b p) d -> p b d", p=P)))
        x_loaded = l_x.dma(S, lambda e: e.dma_start(x_in[0:LAST, NB - 1, :], ins["x"][(NB - 1) * P:N, :]), t_pad)
        vectors = {}
        at = 0
        for name, n in (("L0_gnn_ln1_g", KC), ("L0_gnn_ln1_b", KC), ("L0_gnn_ln2_g", KC), ("L0_gnn_ln2_b", KC),
                        ("L1_gnn_ln_g", KC * LAYERS), ("L1_gnn_ln_b", KC * LAYERS), ("L0_gnn_b1", FC)):
            src = ins[name]
            if len(src.shape) == 2:
                src = src.rearrange("l d -> (l d)")
            vectors_in = l_vec.dma(S, lambda e, at=at, n=n, src=src: e.dma_start(columns_in[at:at + n, :], src.rearrange("(k p) -> k p", p=P)))
            vectors[name] = at
            at += n
        assert at == VECTORS
        column = lambda name, k: columns[:, vectors[name] + k:vectors[name] + k + 1]
        spread = lambda ap: ap.unsqueeze(0).broadcast_to([P, ap.shape[0]])
        w_view = lambda ap: ap.rearrange("(k p) n -> p k n", p=P)
        wide_in = l_wide.dma(S, lambda e: e.dma_start(att_linear, spread(ins["L0_gnn_att"].rearrange("h c -> (h c)"))))
        l_w.dma(S, lambda e: e.dma_start(w_left, w_view(ins["L0_gnn_Wl"])))
        w_loaded = l_w.dma(S, lambda e: e.dma_start(w_right, w_view(ins["L0_gnn_Wr"])))
        l_bias.dma(S, lambda e: e.dma_start(gat_bias, spread(ins["L0_gnn_gat_bias"])))
        bias_in = l_bias.dma(S, lambda e: e.dma_start(b2[:, :], spread(ins["L0_gnn_b2"])))
        w1_loaded = l_w1.dma(S, lambda e: e.dma_start(w1, w_view(ins["L0_gnn_W1"])))

        for k in range(HIGH):
            t_digits = V.do(lambda e, k=k: e.memset(digits[:, k, :], float(k)))
        G.do(lambda e: e.memset(ident[:, :], 0.0), t_pad)
        g1 = G.do(lambda e: e.memset(ones[:, :], 1.0))
        G.do(lambda e: e.affine_select(out=ident[:, :], in_=ident[:, :], compare_op=ALU.not_equal, fill=1.0,
                                       base=0, pattern=[[-1, P]], channel_multiplier=1), g1)
        G.do(lambda e: e.affine_select(out=earlier, in_=ones[:, :], compare_op=ALU.is_ge, fill=0.0,
                                       base=-1, pattern=[[1, P]], channel_multiplier=-1), g1)
        G.do(lambda e: e.iota(iota[:, :], [[1, max(NC, EJ)]], base=0, channel_multiplier=0, allow_small_or_imprecise_dtypes=True))
        G.do(lambda e: e.memset(eps[:, :], LN_EPS))
        G.do(lambda e: e.memset(zero[:, :], 0.0))
        t_const = G.do(lambda e: e.iota(iota_node, [[1, NP]], base=0, channel_multiplier=0, allow_small_or_imprecise_dtypes=True))

        t = T.do(lambda e: e.transpose(bank[:, 7, 0:VECTORS], columns_in[0:VECTORS, :], ident[0:VECTORS, 0:VECTORS]), t_const, vectors_in)
        columns_ready = A.do(lambda e: e.activation(columns[:, :], bank[:, 7, 0:VECTORS], ACT.Copy), t)

        R0 = slice(0, EP)

        def ranks(radix, after, shift_for=None, before_sums=lambda: None, behind_sums=lambda: None):
            m3 = match[R0, 0:radix * EJ].rearrange("p (k j) -> p k j", j=EJ)
            s3 = running[R0, 0:radix * EJ].rearrange("p (k j) -> p k j", j=EJ)
            r3 = ranked[R0, 0:radix * EJ].rearrange("p (k j) -> p k j", j=EJ)
            t = V.do(lambda e: e.tensor_tensor(m3, over(digit[R0, :], 1, radix), digits[R0, 0:radix, :], ALU.is_equal), t_digits, after)
            t = V.do(lambda e: e.tensor_tensor_scan(running[R0, 0:radix * EJ], match[R0, 0:radix * EJ], match[R0, 0:radix * EJ], 0.0, ALU.add, ALU.max), t)
            t1 = V.do(lambda e: e.memset(shifted[R0, 0:1], 0.0))
            t2 = V.do(lambda e: e.tensor_copy(total[R0, 0:radix], s3[:, :, EJ - 1]), t)
            t3 = V.do(lambda e: e.tensor_copy(shifted[R0, 1:radix], s3[:, 0:radix - 1, EJ - 1]))
            t4 = V.do(lambda e: e.tensor_tensor(per_digit[R0, 0:radix], total[R0, 0:radix], shifted[R0, 0:radix], ALU.subtract), t1, t2, t3)
            before_sums()
            T.quiet(lambda e: e.matmul(bank[R0, 6, 0:radix], ones[R0, R0], shifted[R0, 0:radix], start=True, stop=False), t_const, t4)
            t5 = T.do(lambda e: e.matmul(bank[R0, 6, 0:radix], earlier[R0, R0], per_digit[R0, 0:radix], start=False, stop=True))
            behind_sums()
            t6 = V.do(lambda e: e.scalar_tensor_tensor(base_of[R0, 0:radix], bank[R0, 6, 0:radix], -1.0, shifted[R0, 0:radix], ALU.add, ALU.subtract), t5)
            if shift_for is not None:
                t6 = shift_for(t6)
            t7 = V.do(lambda e: e.tensor_tensor(r3, s3, over(base_of[R0, 0:radix], 2, EJ), ALU.add), t6)
            t8 = V.do(lambda e: e.tensor_tensor(r3, r3, m3, ALU.mult), t7)
            return V.do(lambda e: e.tensor_reduce(place[R0, :], r3.rearrange("p k j -> p j k"), AX.X, ALU.add), t8)

        def divide(quotient, value, by, after, remainder=None):
            t = V.do(lambda e: e.tensor_scalar(quotient, value, 1.0 / by, -(by - 1) / 2.0 / by, ALU.mult, ALU.add), after)
            t = V.do(lambda e: e.tensor_scalar(quotient, quotient, ROUND, ROUND, ALU.add, ALU.subtract), t)
            if remainder is None:
                return t
            return V.do(lambda e: e.scalar_tensor_tensor(remainder, quotient, -float(by), value, ALU.mult, ALU.add), t)

        def one_hot(out_ap, gap_ap, iota_ap, minus_ap, *after):
            t = A.do(lambda e: e.activation(gap_ap, iota_ap, ACT.Abs, bias=minus_ap), *after)
            return A.do(lambda e: e.activation(out_ap, gap_ap, ACT.Relu, bias=ones[0:iota_ap.shape[0], 0:1], scale=-1.0), t)

        def permute(out_rows, width, row, col, after, b, between=lambda j: None):
            used, gap_used = [None] * RING, [None] * RING
            negated = V.do(lambda e: e.tensor_scalar(minus_row[R0, :], row[R0, :], -1.0, None, ALU.mult), after)
            for j in range(EJ):
                i = j % RING
                r, c = pick_row[i], pick_col[i]
                if j % 3 == 0:
                    gap_used[i] = t1 = one_hot(r[R0, 0:out_rows], pick_gap[i][R0, 0:out_rows], iota[R0, 0:out_rows], minus_row[R0, j:j + 1], negated, used[i], gap_used[i])
                else:
                    queue = G if j % 3 == 1 else V
                    t1 = queue.do(lambda e, j=j, r=r: e.tensor_scalar(r[R0, 0:out_rows], iota[R0, 0:out_rows], row[R0, j:j + 1], None, ALU.is_equal), after, used[i])
                t = V.do(lambda e, j=j, c=c: e.tensor_scalar(c[R0, 0:width], iota[R0, 0:width], col[R0, j:j + 1], packed[R0, j:j + 1], ALU.is_equal, ALU.mult), after, used[i])
                used[i] = T.do(lambda e, j=j, r=r, c=c: e.matmul(bank[0:out_rows, b, 0:width], r[R0, 0:out_rows], c[R0, 0:width], start=(j == 0), stop=(j == EJ - 1)), t, t1)
                between(j)
            return used[(EJ - 1) % RING]

        norm_turn = [0]
        norm_used = [None] * norm_slots

        def statistics_of(rows_ap, *after):
            s = norm_turn[0] % norm_slots
            norm_turn[0] += 1
            t = V.do(lambda e: e.bn_stats(stat[:, s, :], rows_ap), norm_used[s], *after)
            return s, V.do(lambda e: e.bn_aggr(moments[:, s, :], stat[:, s, :]), t)

        def deviation_of(st):
            s, t = st
            return s, A.do(lambda e: e.activation(deviation[:, s, :], moments[:, s, 1:2], ACT.Sqrt, bias=eps[:, :]), t)

        def moments_of(rows_ap, *after):
            return deviation_of(statistics_of(rows_ap, *after))

        def apply_moments(st, out_ap, rows_ap, *after):
            s, t = st
            t = V.do(lambda e: e.reciprocal(rstd[:, s, :], deviation[:, s, :]), t)
            norm_used[s] = V.do(lambda e: e.tensor_scalar(out_ap, rows_ap, moments[:, s, 0:1], rstd[:, s, :], ALU.subtract, ALU.mult), t, *after)
            return norm_used[s]

        def turn(rows_ap, dest, gain, offset, psum, free, *after):
            for k in range(KC):
                t = T.do(lambda e, k=k: e.transpose(bank[:, psum, k * P:(k + 1) * P], rows_ap[:, k * P:(k + 1) * P], ident[:, :]), *after)
            for k in range(KC):
                done = A.do(lambda e, k=k: e.activation(dest[:, k, :], bank[:, psum, k * P:(k + 1) * P], ACT.Identity,
                                                        bias=column(offset[0], offset[1] + k), scale=column(gain[0], gain[1] + k)), t, columns_ready, free)
            return t, done

        twice = [None] * NB
        ready = {}
        tile_free, tables_written = [None] * 4, []
        l_tile = [landing(f"tile{i}") for i in range(4)]

        def projections():
            bank_free, product_read = {}, [None] * 3
            turned_at = [None] * NB
            psum_free = [columns_ready] * 2

            def turn_block(b):
                _, turned_at[b] = turn(x_in[:, b, :], trans[b % 3], ("L0_gnn_ln1_g", 0), ("L0_gnn_ln1_b", 0), b % 2, product_read[b % 3], twice[b], psum_free[b % 2])
                psum_free[b % 2] = turned_at[b]
            turn_block(0)
            yield
            for b in range(NB):
                if b + 1 < NB:
                    turn_block(b + 1)
                    yield
                for side, (w, table) in enumerate(((w_left, left_table), (w_right, right_table))):
                    n = 2 * b + side
                    for k in range(KC):
                        lhs = trans[b % 3][:, k, :]
                        T.quiet(lambda e, k=k, w=w, lhs=lhs, side=side: e.matmul(bank[:, 2 + side, :], lhs, w[:, k, :], start=(k == 0), stop=(k == KC - 1)), turned_at[b], w_loaded, bank_free.get(side))
                        yield
                    for k in range(KC):
                        lhs = trans[b % 3][:, k, :]
                        t = T.do(lambda e, k=k, side=side, lhs=lhs: e.matmul(bank[:, 4 + side, 0:HEADS], lhs, wa[:, side, k, :], start=(k == 0), stop=(k == KC - 1)), ready["wa"])
                    product_read[b % 3] = t
                    tl = tile[n % 4]
                    A.do(lambda e, tl=tl, side=side: e.activation(tl[:, 0:D], bank[:, 2 + side, :], ACT.Copy), t, tile_free[n % 4])
                    bank_free[side] = A.do(lambda e, tl=tl, side=side: e.activation(tl[:, D:TW], bank[:, 4 + side, 0:HEADS], ACT.Copy))
                    tile_free[n % 4] = l_tile[n % 4].dma(S, lambda e, tl=tl, table=table, b=b: e.dma_start(table[b * P:(b + 1) * P, :], tl), bank_free[side])
                    tables_written.append(tile_free[n % 4])
                    yield

        projecting = projections()
        STEPS = NB + NB * 2 * (KC + 1)
        NORM_STEPS, LOW_STEPS, COLUMN_STEPS, HIGH_STEPS, PLACE_STEPS = 2 + 5 * (NB - 3), 22, 8, 14, 28

        def project(some):
            for _ in range(some):
                next(projecting, None)

        def before_projection():
            t = V.do(lambda e: e.tensor_scalar(att_relu, att_linear, 1.0 - SLOPE, None, ALU.mult), wide_in)
            att_ready = V.do(lambda e: e.tensor_scalar(att_linear, att_linear, SLOPE, None, ALU.mult), t)

            products = [ranked[:, side * KC * D:(side + 1) * KC * D] for side in range(2)]
            multiplied = [G.do(lambda e, p=p, w=w: e.tensor_tensor(p.rearrange("p (k n) -> p k n", n=D), w, over(att_linear, 1, KC), ALU.mult), w_loaded, att_ready)
                          for p, w in zip(products, (w_left, w_right))]

            first = moments_of(x_in[:, 0, :], x_loaded)
            for b in range(NB):
                t = apply_moments(first, x_in[:, b, :], x_in[:, b, :])
                if b + 1 < NB:
                    first = moments_of(x_in[:, b + 1, :])
                t = V.do(lambda e, b=b: e.tensor_scalar(state[:, b, :], x_in[:, b, :], 0.0, None, ALU.max), t)
                second = moments_of(state[:, b, :], t)
                if b:
                    twice[b - 1] = apply_moments(before, x_in[:, b - 1, :], state[:, b - 1, :])
                before = second
                if b == 2:
                    for side in range(2):
                        ready["wa"] = V.do(lambda e, side=side: e.tensor_reduce(wa[:, side, :, :].rearrange("p k h -> p (k h)"), products[side].rearrange("p (r c) -> p r c", c=C), AX.X, ALU.add), multiplied[side])
                if b:
                    project(1 if b < 3 else 5)
            twice[NB - 1] = apply_moments(before, x_in[:, NB - 1, :], state[:, NB - 1, :])
            for b in range(NB):
                ready["state"] = G.do(lambda e, b=b: e.tensor_tensor(state[:, b, :], state[:, b, :], gat_bias, ALU.add), twice[b], bias_in)

        t1 = V.do(lambda e: e.tensor_copy(src_g[R0, :], src_in[R0, :]), edges_in)
        t2 = V.do(lambda e: e.tensor_copy(dst_g[R0, :], dst_in[R0, :]))
        t3 = V.do(lambda e: e.tensor_scalar(digit_i[R0, :], dst_in[R0, :], LOW - 1, None, ALU.bitwise_and))
        V.do(lambda e: e.scalar_tensor_tensor(packed[R0, :], dst_g[R0, :], float(PACK), src_g[R0, :], ALU.mult, ALU.add), t1, t2)
        t4 = V.do(lambda e: e.tensor_copy(digit[R0, :], digit_i[R0, :]), t3)

        def beside_low():
            before_projection()
            project(LOW_STEPS)
        t = ranks(LOW, t4, behind_sums=beside_low)
        low_ready = divide(place_hi[R0, :], place[R0, :], EJ, t, place_lo[R0, :])

        def spread_over_columns(steps):
            return lambda j: project(1) if (j + 1) * steps // EJ > j * steps // EJ else None
        low_sorted = permute(EP, EJ, place_hi, place_lo, low_ready, 6, spread_over_columns(COLUMN_STEPS))

        t = V.do(lambda e: e.tensor_copy(packed[R0, :], bank[R0, 6, 0:EJ]), low_sorted)
        t1 = V.do(lambda e: e.tensor_copy(digit_i[R0, :], packed[R0, :]), t)
        t1 = V.do(lambda e: e.tensor_scalar(digit_i[R0, :], digit_i[R0, :], (PACK * LOW).bit_length() - 1, None, ALU.arith_shift_right), t1)
        t1 = V.do(lambda e: e.tensor_copy(digit[R0, :], digit_i[R0, :]), t1)
        V.do(lambda e: e.tensor_scalar(packed[R0, :], packed[R0, :], float(PACK), None, ALU.add), t)

        def pad_blocks(after):
            t = T.do(lambda e: e.matmul(bank[:, 7, 0:HIGH], ones[R0, :], total[R0, 0:HIGH], start=True, stop=True), after, columns_ready)
            t = V.do(lambda e: e.tensor_copy(block_end, bank[:, 7, 0:HIGH].rearrange("p (b q) -> p b q", q=HPB)[:, :, HPB - 1]), t)
            t1 = V.do(lambda e: e.memset(block_before[:, 0:1], 0.0))
            t2 = V.do(lambda e: e.tensor_copy(block_before[:, 1:NB], block_end[:, 0:NB - 1]), t)
            t = V.do(lambda e: e.tensor_tensor(block_n, block_end, block_before, ALU.subtract), t1, t2)
            t = V.do(lambda e: e.tensor_scalar(block_n, block_n, float(PAIR - 1), None, ALU.add), t)
            t = divide(pairs, block_n, PAIR, t)
            t = V.do(lambda e: e.tensor_tensor_scan(pair_end, pairs, pairs, 0.0, ALU.add, ALU.max), t)
            t = V.do(lambda e: e.tensor_tensor(pair_at, pair_end, pairs, ALU.subtract), t)
            t = V.do(lambda e: e.scalar_tensor_tensor(shift, pair_at, float(PAIR), block_before, ALU.mult, ALU.subtract), t)
            b3 = base_of[R0, 0:HIGH].rearrange("p (b q) -> p b q", q=HPB)
            out_t = V.do(lambda e: e.tensor_tensor(b3, b3, over(shift[R0, :], 2, HPB), ALU.add), t)
            p3 = passed.rearrange("p (g b) -> p g b", b=NB - 1)
            t = V.do(lambda e: e.tensor_tensor(p3, over(pair_at[:, 1:NB], 1, NG), over(iota[:, 0:NG], 2, NB - 1), ALU.is_le), t)
            t = V.do(lambda e: e.tensor_reduce(block_f, p3, AX.X, ALU.add), t)
            V.do(lambda e: e.tensor_copy(block_of[:, :], block_f[0:1, :]), t)
            return out_t

        t = ranks(HIGH, t1, pad_blocks, before_sums=lambda: project(HIGH_STEPS))
        V.do(lambda e: e.tensor_reduce(is_head[:, :], ident[:, :].rearrange("p (g h) -> p h g", h=HEADS), AX.X, ALU.add), t_const)
        V.do(lambda e: e.tensor_reduce(is_run[:, :], ident[:, :].rearrange("p (g h) -> p g h", h=HEADS), AX.X, ALU.add))
        V.do(lambda e: e.tensor_copy(to_rows[:, :].rearrange("q (g h) -> q g h", h=HEADS), over(ident[0:HEADS, 0:HEADS], 1, SG)))
        high_ready = divide(place_hi[R0, :], place[R0, :], P, t, place_lo[R0, :])
        project(PLACE_STEPS)
        behind_projection = spread_over_columns(STEPS - NORM_STEPS - LOW_STEPS - COLUMN_STEPS - HIGH_STEPS - PLACE_STEPS)

        def zero_counts(blocks, after):
            return A.do(lambda e: e.activation(counts[:, blocks, :], zero[:, 0:1].unsqueeze(2).broadcast_to([P, blocks.stop - blocks.start, NP]), ACT.Copy), after)

        def beside_high(j):
            behind_projection(j)
            b, between = divmod(j, EJ // EARLY_ZEROS)
            if between == 0 and b < EARLY_ZEROS:
                zero_counts(slice(b, b + 1), high_ready)
        t = permute(P, NC, place_lo, place_hi, high_ready, 6, beside_high)
        project(STEPS)
        t = V.do(lambda e: e.tensor_copy(slots_i, bank[:, 6, 0:NC]), t)
        V.do(lambda e: e.tensor_scalar(src_of[:, :], slots_i, PACK - 1, None, ALU.bitwise_and), t)
        t1 = V.do(lambda e: e.tensor_scalar(part_i, slots_i, PACK.bit_length() - 1, None, ALU.arith_shift_right))
        V.do(lambda e: e.tensor_copy(src_f[:, :], src_of[:, :]), t1)
        t = V.do(lambda e: e.tensor_copy(key[:, :], part_i), t1)
        V.do(lambda e: e.tensor_scalar(dst_of[:, :], key[:, :], -1.0, 0.0, ALU.add, ALU.max), t)
        l3 = local[:, :].rearrange("p (g i) -> p g i", i=2)
        t = V.do(lambda e: e.scalar_tensor_tensor(l3, over(block_f, 2, 2), -float(P), key[:, :].rearrange("p (g i) -> p g i", i=2), ALU.mult, ALU.add), t)
        t = V.do(lambda e: e.tensor_scalar(local[:, :], local[:, :], -1.0, None, ALU.add), t)
        slots_ready = V.do(lambda e: e.tensor_scalar(minus_local, local, -1.0, None, ALU.mult), t)
        counts_zero = zero_counts(slice(EARLY_ZEROS, NB), slots_ready)

        DEPTH = 6
        plan = Plan(0, W1_AT - EARLY)
        gathered = [plan.take(2, TW) for _ in range(DEPTH)]
        weighted = [plan.take(2, D) for _ in range(2)]
        score = plan.take(NC, HEADS)
        hot_at = plan.at
        src_hot = [plan.take(NP, dt=BF16) for _ in range(4)]
        dst_hot = [plan.take(P, dt=BF16) for _ in range(4)]
        src_gap = [plan.take(NP, dt=BF16) for _ in range(2)]
        dst_gap = [plan.take(P, dt=BF16) for _ in range(4)]
        hot_end = plan.at
        minus_src = plan.take(NC)
        weights = plan.take(NC, HEADS + 1)
        hot = [plan.take(P) for _ in range(4)]
        gap = [plan.take(P) for _ in range(4)]
        agg_at = plan.at
        agg = plan.take(NB, D)
        agg_den = plan.take(NB, HEADS + 1)
        agg_end = plan.at

        plan = Plan(agg_at, agg_end)
        turned_key = plan.take(RUN)
        reset = plan.take(RUN)
        not_first, not_last = plan.take(RUN, dt=BF16), plan.take(RUN, dt=BF16)
        ends = plan.take(4 * SG)
        small = plan.take(9 * SG)
        carry_rows = plan.take(2 * SG)
        carry = plan.take(2)
        key_rows = Plan(DEPTH * 2 * TW).take(SK, P)
        t = V.do(lambda e: e.memset(weights[:, :, HEADS], 1.0), slots_ready, *tables_written[-4:])
        V.do(lambda e: e.tensor_scalar(minus_src, src_f, -1.0, None, ALU.mult))
        buffers_ready = V.do(lambda e: e.tensor_copy(key_rows.rearrange("p k (g h) -> p k g h", h=HEADS), over(key.rearrange("p (g k) -> p k g", k=SK), 3, HEADS)))
        for k in range(SK):
            keys_turned = T.do(lambda e, k=k: e.transpose(flat[:, k * P:(k + 1) * P], key_rows[:, k, :], ident[:, :]), buffers_ready)

        l_gather = [landing(f"gather{i}") for i in range(DEPTH)]
        l_add = [landing(f"add{i}") for i in range(DEPTH)]
        gather_free = [slots_ready] * DEPTH
        own = [None] * DEPTH

        def gather(lands, table, index, g, i, add, *after):
            extra = dict(compute_op=ALU.add, bounds_check=NP - 1, oob_is_err=True) if add else {}
            c = 2 * g + i
            return lands.dma(G, lambda e: e.indirect_dma_start(
                out=gathered[g % DEPTH][:, i, :], out_offset=None, in_=table,
                in_offset=bass.IndirectOffsetOnAxis(ap=index[:, c:c + 1], axis=0), **extra), *after)

        def gather_left(g):
            for i in range(2):
                own[g % DEPTH] = gather(l_gather[g % DEPTH], left_table, src_of, g, i, False, gather_free[g % DEPTH], *tables_written[-4:])

        AHEAD = 3
        for g in range(AHEAD):
            gather_left(g)

        t1 = V.do(lambda e: e.tensor_copy(turned_key, flat[:, 0:RUN]), keys_turned)
        V.do(lambda e: e.memset(reset[:, 0:1], 0.0))
        t = V.do(lambda e: e.tensor_tensor(reset[:, 1:RUN], turned_key[:, 1:RUN], turned_key[:, 0:RUN - 1], ALU.not_equal), t1)
        V.do(lambda e: e.tensor_scalar(reset[:, 1:RUN], reset[:, 1:RUN], FAR, None, ALU.mult), t)
        first_of_run, last_of_run = turned_key[:, 0:1], turned_key[:, RUN - 1:RUN]
        V.do(lambda e: e.tensor_scalar(not_first, turned_key, first_of_run, FAR, ALU.not_equal, ALU.mult))
        V.do(lambda e: e.tensor_scalar(not_last, turned_key, last_of_run, FAR, ALU.not_equal, ALU.mult))

        def spread_end(n, col, *after):
            return V.do(lambda e: e.tensor_scalar(ends[:, n * SG:(n + 1) * SG], is_run[:, :], col, None, ALU.mult), *after)
        spread_end(2, first_of_run)
        resets_ready = spread_end(3, last_of_run)

        weighted_free, hot_free, src_gap_free, dst_gap_free = [None] * 2, [None] * 4, [None] * 2, [None] * 4
        count_free = [t1, counts_zero]

        def source_hot(g):
            s = 2 * g % 4
            src_ready[g] = V.do(lambda e: e.tensor_scalar(src_hot[s], iota_node, src_f[:, 2 * g:2 * g + 1], None, ALU.is_equal), hot_free[s])
        src_ready = {}

        def count_pair(g):
            lo = 3 * (g % 2)
            for i in range(2):
                c = 2 * g + i
                s = c % 4
                if i == 0:
                    src_t = src_ready[g]
                else:
                    src_t = one_hot(src_hot[s], src_gap[g % 2], iota_node, minus_src[:, c:c + 1], src_gap_free[g % 2], hot_free[s], buffers_ready)
                    src_gap_free[g % 2] = src_t
                dst_t = one_hot(dst_hot[s], dst_gap[s], iota_node[:, 0:P], minus_local[:, c:c + 1], dst_gap_free[s], hot_free[s], buffers_ready)
                dst_gap_free[s] = dst_t
                for b in range(NB):
                    o = flat[:, lo * 512 + b * P:lo * 512 + (b + 1) * P]
                    f = lambda e, s=s, b=b, o=o, i=i: e.matmul(o, src_hot[s][:, b * P:(b + 1) * P], dst_hot[s], start=(i == 0 and b % 4 == 0), stop=(i == 1), skip_group_check=True)
                    if b < NB - 1:
                        T.quiet(f, src_t, dst_t, count_free[g % 2])
                    else:
                        hot_free[s] = T.do(f)
            return hot_free[(2 * g + 1) % 4]

        block_number = {}

        def load_block_number(g):
            def fn(e):
                block_number[g] = e.value_load(block_of[0:1, g:g + 1], min_val=0, max_val=NB - 1)
            V.quiet(fn)

        def add_counts(g, ready):
            lo = 3 * (g % 2)

            def fn(e):
                d = counts[:, :, bass.ds(block_number[g] * P, P)]
                return e.tensor_tensor(d, d, flat[:, lo * 512:lo * 512 + NP].rearrange("p (b n) -> p b n", n=P), ALU.add)
            count_free[g % 2] = V.do(fn, ready, counts_zero, count_free[(g + 1) % 2])

        source_hot(0)
        counted = None
        for g in range(NG):
            s = g % DEPTH
            if g + AHEAD < NG:
                gather_left(g + AHEAD)
            for i in range(2):
                t = gather(l_add[s], right_table, dst_of, g, i, True, own[s])
            counting = count_pair(g)
            w = weighted[g % 2]
            t1 = V.do(lambda e, s=s, w=w: e.scalar_tensor_tensor(w, gathered[s][:, :, 0:D], 0.0, over(att_relu, 1, 2), ALU.max, ALU.mult), t, weighted_free[g % 2])
            if g:
                load_block_number(g - 1)
                add_counts(g - 1, counted)
            sc = score[:, 2 * g:2 * g + 2, :]
            t1 = V.do(lambda e, w=w, sc=sc: e.tensor_reduce(sc.rearrange("p i h -> p (i h)"), w.rearrange("p i (h c) -> p (i h) c", c=C), AX.X, ALU.add), t1)
            weighted_free[g % 2] = t1
            if g + 1 < NG:
                source_hot(g + 1)
            gather_free[s] = V.do(lambda e, s=s, sc=sc: e.tensor_tensor(sc, sc, gathered[s][:, :, D:TW], ALU.add), t1)
            counted = counting
        load_block_number(NG - 1)
        add_counts(NG - 1, counted)
        scores_ready = gather_free[(NG - 1) % DEPTH]

        l_again = [landing(f"again{i}") for i in range(DEPTH)]
        landed = [None] * DEPTH

        def gather_again(g):
            for i in range(2):
                landed[g % DEPTH] = gather(l_again[g % DEPTH], left_table, src_of, g, i, False, gather_free[g % DEPTH])
        for g in range(DEPTH - 1):
            gather_again(g)

        plan = Plan(hot_at, hot_end)
        behind_max = plan.take(RUN)
        turned = plan.take(RUN)
        ahead_max = turned_key
        score_rows = Plan(DEPTH * 2 * TW).take(SK, P)
        t2 = V.do(lambda e: e.tensor_copy(score_rows.rearrange("p k (g h) -> p k g h", h=HEADS), score.rearrange("p (g k) h -> p k g h", k=SK)), scores_ready)
        for k in range(SK):
            ts = T.do(lambda e, k=k: e.transpose(flat[:, k * P:(k + 1) * P], score_rows[:, k, :], ident[:, :]), t2, count_free[0], count_free[1])
        t2 = V.do(lambda e: e.tensor_copy(turned, flat[:, 0:RUN]), ts)
        t5 = V.do(lambda e: e.tensor_tensor_scan(ahead_max, reset, turned, FAR, ALU.add, ALU.max), t2, resets_ready)
        t6 = V.do(lambda e: e.tensor_copy(behind_max[:, RUN - 1:RUN], turned[:, RUN - 1:RUN]))
        t7 = V.do(lambda e: e.tensor_tensor_scan(behind_max[:, 0:RUN - 1][:, ::-1], reset[:, 1:RUN][:, ::-1], turned[:, 0:RUN - 1][:, ::-1],
                                                 turned[:, RUN - 1:RUN], ALU.add, ALU.max), t6)
        spread_end(0, ahead_max[:, RUN - 1:RUN], t5)
        t = spread_end(1, behind_max[:, 0:1], t7)
        t = T.do(lambda e: e.matmul(bank[0:HEADS, 6, 0:4 * SG], is_head[:, :], ends, start=True, stop=True), t)
        H8 = slice(0, HEADS)
        right_end, left_end, first_key, last_key, wall, wall_b, over_f, chain_f, chain_b = [small[H8, i * SG:(i + 1) * SG] for i in range(9)]
        t = V.do(lambda e: e.tensor_copy(small[H8, 0:4 * SG], bank[0:HEADS, 6, 0:4 * SG]), t)
        carry_f, carry_b = carry_rows[H8, 0:SG], carry_rows[H8, SG:2 * SG]

        def walls(dest, one, other, *after):
            t = V.do(lambda e: e.tensor_tensor(dest, one, other, ALU.not_equal), *after)
            return V.do(lambda e: e.tensor_scalar(dest, dest, FAR, None, ALU.mult), t)
        V.do(lambda e: e.memset(small[H8, 4 * SG:7 * SG], 0.0))
        t0 = V.do(lambda e: e.memset(carry_rows[H8, :], FAR))
        ta = walls(wall[:, 1:SG], last_key[:, 1:SG], last_key[:, 0:SG - 1], t, t0)
        tb = walls(wall_b[:, 0:SG - 1], first_key[:, 0:SG - 1], first_key[:, 1:SG])
        tc = walls(over_f[:, 1:SG], first_key[:, 1:SG], last_key[:, 0:SG - 1])
        ta = V.do(lambda e: e.tensor_tensor_scan(chain_f, wall, right_end, FAR, ALU.add, ALU.max), ta)
        tb = V.do(lambda e: e.tensor_tensor_scan(chain_b[:, ::-1], wall_b[:, ::-1], left_end[:, ::-1], FAR, ALU.add, ALU.max), tb)
        V.do(lambda e: e.tensor_tensor(carry_f[:, 1:SG], chain_f[:, 0:SG - 1], over_f[:, 1:SG], ALU.add), ta, tc)
        t = V.do(lambda e: e.tensor_tensor(carry_b[:, 0:SG - 1], chain_b[:, 1:SG], over_f[:, 1:SG], ALU.add), tb)
        t = T.do(lambda e: e.matmul(bank[:, 6, 128:128 + 2 * SG], to_rows[:, :], carry_rows[H8, :], start=True, stop=True), t)
        c3 = ends[:, 0:2 * SG].rearrange("p (w g) -> p w g", w=2)
        t = V.do(lambda e: e.tensor_tensor(c3, bank[:, 6, 128:128 + 2 * SG].rearrange("p (w g) -> p w g", w=2), over(is_run[:, :], 1, 2), ALU.mult), t)
        t = V.do(lambda e: e.tensor_reduce(carry, c3, AX.X, ALU.add), t)
        V.do(lambda e: e.scalar_tensor_tensor(ahead_max, not_first, carry[:, 0:1], ahead_max, ALU.add, ALU.max), t)
        m2 = V.do(lambda e: e.scalar_tensor_tensor(behind_max, not_last, carry[:, 1:2], behind_max, ALU.add, ALU.max))
        t = V.do(lambda e: e.tensor_tensor(ahead_max, ahead_max, behind_max, ALU.max), m2)
        max_ready = V.do(lambda e: e.tensor_tensor(turned, turned, ahead_max, ALU.subtract), t)
        t = A.do(lambda e: e.activation(turned, turned, ACT.Exp), max_ready)
        for k in range(SK):
            tw = T.do(lambda e, k=k: e.transpose(flat[:, k * P:(k + 1) * P], turned[:, k * P:(k + 1) * P], ident[:, :]), t)
        V.do(lambda e: e.memset(agg, 0.0), max_ready)
        agg_zero = V.do(lambda e: e.memset(agg_den, 0.0))
        w4 = weights[:, :, 0:HEADS].rearrange("p (g k) h -> p k g h", k=SK)
        weights_ready = V.do(lambda e: e.tensor_copy(w4, flat[:, 0:RUN].rearrange("p (k g h) -> p k g h", g=SG, h=HEADS)), tw)

        hot_free, gap_free = [None] * 4, [None] * 4
        weighted_free = [weights_ready] * 2
        SUMS = 4
        sum_free = [agg_zero] * SUMS

        summed_at = {}

        def add_sums(g):
            b0 = g % SUMS

            def both(e):
                r = block_number[g]
                d = agg[:, bass.ds(r, 1), :].rearrange("p b n -> p (b n)")
                e.tensor_tensor(d, d, bank[:, b0, :], ALU.add).then_inc(V.sem, 1)
                d = agg_den[:, bass.ds(r, 1), :].rearrange("p b n -> p (b n)")
                return e.tensor_tensor(d, d, bank[:, SUMS + b0, 0:HEADS + 1], ALU.add)
            V.count += 1
            sum_free[b0] = V.do(both, summed_at[g], sum_free[(g - 1) % SUMS])

        for g in range(NG):
            s = g % DEPTH
            w = weighted[g % 2]
            msg_t = V.do(lambda e, s=s, w=w, g=g: e.tensor_tensor(
                w.rearrange("p i (h c) -> p i h c", c=C), gathered[s][:, :, 0:D].rearrange("p i (h c) -> p i h c", c=C),
                over(weights[:, 2 * g:2 * g + 2, 0:HEADS], 3, C), ALU.mult), landed[s], weighted_free[g % 2])
            gather_free[s] = msg_t
            if g > 1:
                load_block_number(g - 2)
            if g + DEPTH - 1 < NG:
                gather_again(g + DEPTH - 1)
            for i in range(2):
                c = 2 * g + i
                h = hot[c % 4]
                hot_t = one_hot(h, gap[c % 4], iota[:, 0:P], minus_local[:, c:c + 1], gap_free[c % 4], hot_free[c % 4])
                gap_free[c % 4] = hot_t
                T.quiet(lambda e, h=h, w=w, i=i, g=g: e.matmul(bank[:, g % SUMS, :], h, w[:, i, :], start=(i == 0), stop=(i == 1)), msg_t, hot_t, sum_free[g % SUMS])
                hot_free[c % 4] = T.do(lambda e, h=h, c=c, i=i, g=g: e.matmul(bank[:, SUMS + g % SUMS, 0:HEADS + 1], h, weights[:, c, :], start=(i == 0), stop=(i == 1)))
            weighted_free[g % 2] = summed_at[g] = hot_free[(2 * g + 1) % 4]
            if g > 1:
                add_sums(g - 2)
        for g in (NG - 2, NG - 1):
            load_block_number(g)
            add_sums(g)
        sums_done = sum_free[(NG - 1) % SUMS]

        as_float = lambda ap: ap.bitcast(F32)
        COLS = GROUP * P
        w2 = Plan(0).take(FC, D)
        plan = Plan(FC * D, W1_AT)
        turned_hi, turned_lo = [None] * 2, [None] * 2
        turned_hi[0], turned_lo[0] = plan.rounded("turned_hi0", KC, COLS), plan.rounded("turned_lo0", KC, COLS)
        w1_hi = [plan.rounded(f"w1_hi{i}", KC, P) for i in range(2)]
        w1_lo = [plan.rounded(f"w1_lo{i}", KC, P) for i in range(2)]
        w2_hi = [plan.rounded(f"w2_hi{i}", D) for i in range(2)]
        w2_lo = [plan.rounded(f"w2_lo{i}", D) for i in range(2)]
        assert plan.at <= agg_at
        hidden = [plan.take(COLS) for _ in range(2)]
        hidden_hi = [plan.rounded(f"hidden_hi{i}", COLS) for i in range(2)]
        hidden_lo = [plan.rounded(f"hidden_lo{i}", COLS) for i in range(2)]
        second_at = plan.at
        turned_hi[1], turned_lo[1] = plan.rounded("turned_hi1", KC, COLS), plan.rounded("turned_lo1", KC, COLS)
        assert agg_end <= plan.at
        rows2 = [plan.take(D) for _ in range(2)]
        x_again = plan.take(D)
        turned_f = plan.take(KC, P)

        w2_parts = [0, 1, 4, 10, FC]
        w2_loaded = [None] * FC
        w2_rows = w_view(ins["L0_gnn_W2"])
        for i, (f0, f1) in enumerate(zip(w2_parts, w2_parts[1:])):
            t = landing(f"w2_{i}").dma(S, lambda e, f0=f0, f1=f1: e.dma_start(w2[:, f0:f1, :], w2_rows[:, f0:f1, :]), weighted_free[(NG - 1) % 2], sums_done)
            w2_loaded[f0:f1] = [t] * (f1 - f0)

        in_degree = V.do(lambda e: e.tensor_scalar(norm_dst[:, :], agg_den[:, :, HEADS], 1.0, None, ALU.max), sums_done)
        t = V.do(lambda e: e.tensor_scalar(agg_den, agg_den, 1e-16, None, ALU.add), in_degree)
        den_ready = V.do(lambda e: e.reciprocal(agg_den, agg_den), t)
        normed, turned_b, evacuated = [None] * NB, [None] * NB, [None] * NB
        rows_read = [None] * 2
        turn_free = [weights_ready] * 2
        slot_read = [None] * 2

        def add_attention(queue, b):
            a3 = agg[:, b, :].rearrange("p (h c) -> p h c", c=C)
            t = queue.do(lambda e: e.tensor_tensor(a3, a3, over(agg_den[:, b, 0:HEADS], 2, C), ALU.mult), den_ready)
            return queue.do(lambda e: e.tensor_tensor(state[:, b, :], state[:, b, :], agg[:, b, :], ALU.add), t, ready["state"])

        def place_of(b, halves):
            q = b % GROUP
            return halves[b // GROUP % 2][:, :, q * P:(q + 1) * P]

        def turn_rows(b):
            last_lo = turned_b[b - 1] if b else None
            rows_read[b % 2], t = turn(rows2[b % 2], turned_f, ("L0_gnn_ln2_g", 0), ("L0_gnn_ln2_b", 0), 6 + b % 2, last_lo, turn_free[b % 2], normed[b])
            turn_free[b % 2] = t
            evacuated[b] = A.do(lambda e: e.activation(place_of(b, turned_hi), turned_f, ACT.Copy), t, slot_read[b // GROUP % 2], *agg_read)

        def small_part(b):
            turned_b[b] = V.do(lambda e: e.tensor_tensor(place_of(b, turned_lo), turned_f, as_float(place_of(b, turned_hi)), ALU.subtract), evacuated[b], *agg_read)

        rest_ready = [None] * NB
        l_x2 = landing("x_again")

        def add_rest(b):
            n = min(P, N - b * P)
            t = G.do(lambda e: e.tensor_tensor(state[:, b, :], state[:, b, :], b2[:, :], ALU.add), normed[b])
            again = l_x2.dma(S, lambda e: e.dma_start(x_again[0:n, :], ins["x"][b * P:b * P + n, :]), rest_ready[b - 1] if b else sums_done)
            rest_ready[b] = G.do(lambda e: e.tensor_tensor(state[0:n, b, :], state[0:n, b, :], x_again[0:n, :], ALU.add), again, t)

        agg_read = ()
        x1_ready = {b: add_attention(G, b) for b in range(GROUP, NB)}
        ahead = moments_of(state[:, 0, :], add_attention(V, 0))
        for b in range(GROUP):
            st = ahead
            if b + 1 < GROUP:
                x1_ready[b + 1] = add_attention(V, b + 1)
            ahead = moments_of(state[:, b + 1, :], x1_ready[b + 1])
            normed[b] = apply_moments(st, rows2[b % 2], state[:, b, :], rows_read[b % 2], sums_done)
            if b:
                small_part(b - 1)
            turn_rows(b)
            add_rest(b)
        small_part(GROUP - 1)
        agg_read = (x1_ready[GROUP - 1], x1_ready[NB - 1])

        def rows_behind():
            st = {GROUP: ahead}
            for b in range(GROUP + 1, NB):
                st[b] = moments_of(state[:, b, :], x1_ready[b])
            for b in range(GROUP, NB):
                normed[b] = apply_moments(st[b], rows2[b % 2], state[:, b, :], rows_read[b % 2])
                yield
                turn_rows(b)
                add_rest(b)
                small_part(b)
        behind = rows_behind()

        x2_ready = [None] * NB
        norms = {}

        def degree_steps():
            for b in range(NB):
                t = V.do(lambda e, b=b: e.tensor_reduce(norm_src[:, b:b + 1], counts[:, b, :], AX.X, ALU.add), count_free[0], count_free[1])
                yield
            for b in range(NB):
                t1 = V.do(lambda e, b=b: e.tensor_reduce(most[:, b:b + 1], counts[:, b, :], AX.X, ALU.max))
                yield
            t = V.do(lambda e: e.tensor_scalar(norm_src[:, :], norm_src[:, :], 1.0, None, ALU.max), t)
            A.do(lambda e: e.activation(norm_src[:, :], norm_src[:, :], ACT.Sqrt), t)
            t = A.do(lambda e: e.activation(norm_dst[:, :], norm_dst[:, :], ACT.Sqrt), in_degree)
            V.do(lambda e: e.reciprocal(norm_src[:, :], norm_src[:, :]), t)
            norms["ready"] = V.do(lambda e: e.reciprocal(norm_dst[:, :], norm_dst[:, :]))
            t = T.do(lambda e: e.transpose(bank[0:NB, 7, 0:P], most[:, :], ident[:, :]), t1, turned_b[NB - 1])
            t = V.do(lambda e: e.tensor_reduce(most_row[:, :], bank[0:NB, 7, 0:P], AX.X, ALU.max), t)
            yield
            t = T.do(lambda e: e.transpose(bank[0:1, 7, P:P + NB], most_row[:, :], ident[0:NB, 0:NB]), t)
            t = V.do(lambda e: e.tensor_reduce(most_of_all[:, :], bank[0:1, 7, P:P + NB], AX.X, ALU.max), t)
            norms["flag"] = V.do(lambda e: e.tensor_scalar(exact_flag[:, :], most_of_all[:, :], EXACT, None, ALU.is_le), t)
            yield
        degrees = degree_steps()

        def by_flag(e, exact, otherwise):
            e.cond(e.value_load(exact_flag[0:1, 0:1], min_val=0, max_val=1), exact, otherwise)

        steps = [(g0, f) for g0 in range(0, NB, GROUP) for f in range(FC)]
        blocks_of = lambda g0: range(g0, min(NB, g0 + GROUP))
        w1_free, w2_free, hid_free, split_free, out_free = [None] * 2, [None] * 2, [None] * 2, [None] * 2, [None] * GROUP
        w1_ready, w2_ready, hidden_at, small_hidden, summed = {}, {}, {}, {}, {}

        def split_w1(n):
            s, f = n % 2, steps[n][1]
            part = w1[:, :, f * P:(f + 1) * P]
            t = A.do(lambda e: e.activation(w1_hi[s], part, ACT.Copy), w1_loaded, w1_free[s], sums_done)
            w1_ready[n] = V.do(lambda e: e.tensor_tensor(w1_lo[s], part, as_float(w1_hi[s]), ALU.subtract), t)

        def split_w2(n):
            s, f = n % 2, steps[n][1]
            t = A.do(lambda e: e.activation(w2_hi[s], w2[:, f, :], ACT.Copy), w2_loaded[f], w2_free[s])
            w2_ready[n] = V.do(lambda e: e.tensor_tensor(w2_lo[s], w2[:, f, :], as_float(w2_hi[s]), ALU.subtract), t)

        def three(one, other):
            (one_hi, one_lo), (other_hi, other_lo) = one, other
            return (one_hi, other_hi), (one_lo, other_hi), (one_hi, other_lo)

        def hidden_product(n):
            s, (g0, f) = n % 2, steps[n]
            cols, slot = len(blocks_of(g0)) * P, g0 // GROUP % 2
            terms = [(a, b, k) for a, b in three((w1_hi[s], w1_lo[s]), (turned_hi[slot], turned_lo[slot])) for k in range(KC)]
            for i, (a, b, k) in enumerate(terms):
                t = T.do(lambda e, a=a, b=b, k=k, i=i: e.matmul(bank[:, s, 0:cols], a[:, k, :], b[:, k, 0:cols], start=(i == 0), stop=(i == len(terms) - 1)),
                         w1_ready[n], turned_b[blocks_of(g0)[-1]], hid_free[s])
            w1_free[s] = slot_read[slot] = t
            hidden_at[n] = t

        def activate(n):
            s, (g0, f) = n % 2, steps[n]
            cols = len(blocks_of(g0)) * P
            hid_free[s] = A.do(lambda e: e.activation(hidden[s][:, 0:cols], bank[:, s, 0:cols], ACT.Gelu, bias=column("L0_gnn_b1", f)), hidden_at[n], *agg_read, small_hidden.get(n - 2))
            t = A.do(lambda e: e.activation(hidden_hi[s][:, 0:cols], hidden[s][:, 0:cols], ACT.Copy), hid_free[s], split_free[s])
            small_hidden[n] = V.do(lambda e: e.tensor_tensor(hidden_lo[s][:, 0:cols], hidden[s][:, 0:cols], as_float(hidden_hi[s][:, 0:cols]), ALU.subtract), t)

        def output_product(n):
            s, (g0, f) = n % 2, steps[n]
            terms = three((hidden_hi[s], hidden_lo[s]), (w2_hi[s], w2_lo[s]))
            for q, b in enumerate(blocks_of(g0)):
                rows = min(P, N - b * P)
                for i, (a, w) in enumerate(terms):
                    t = T.do(lambda e, a=a, w=w, i=i, q=q, rows=rows: e.matmul(bank[0:rows, 2 + q, :], a[:, q * P:q * P + rows], w, start=(f == 0 and i == 0), stop=(f == FC - 1 and i == len(terms) - 1)),
                             small_hidden[n], w2_ready[n], out_free[q])
            w2_free[s] = split_free[s] = t
            if f == FC - 1:
                summed[g0] = t

        def add_output(g0):
            for q, b in enumerate(blocks_of(g0)):
                rows = min(P, N - b * P)
                out_free[q] = V.do(lambda e, q=q, b=b, rows=rows: e.tensor_tensor(state[0:rows, b, :], state[0:rows, b, :], bank[0:rows, 2 + q, :], ALU.add), summed[g0], rest_ready[b])

        def moments_behind(g0):
            st = {}
            for q, b in enumerate(blocks_of(g0)):
                st[b] = statistics_of(state[:, b, :], out_free[q])
                if q % 2:
                    yield
            st = {b: deviation_of(st[b]) for b in st}
            yield
            for b, (m, t) in st.items():
                t = V.do(lambda e, m=m, b=b: e.reciprocal(x2_scale[:, b:b + 1], deviation[:, m, :]), t)
                x2_ready[b] = norm_used[m] = V.do(lambda e, m=m, b=b: e.scalar_tensor_tensor(x2_shift[:, b:b + 1], moments[:, m, 0:1], -1.0, x2_scale[:, b:b + 1], ALU.mult, ALU.mult), t)
            yield
        behind_moments = iter(())

        split_w1(0)
        hidden_product(0)
        split_w2(0)
        split_w1(1)

        def run_steps(first, last):
            nonlocal behind_moments
            for n in range(first, last):
                g0, f = steps[n]
                activate(n)
                if f == 0 and g0:
                    add_output(g0 - GROUP)
                if n == 0 or (n - 1) % FC < GROUP:
                    next(behind, None)
                if n + 2 < len(steps):
                    split_w1(n + 2)
                split_w2(n + 1)
                hidden_product(n + 1)
                output_product(n)
                if f == 0 and g0:
                    behind_moments = moments_behind(g0 - GROUP)
                next(behind_moments, None)
                if n > GROUP:
                    next(degrees, None)
        LAST_STEP = len(steps) - 1
        run_steps(0, 2 * FC)

        G.wait(norms["flag"])
        G.count += 1
        G.ops.append(lambda e: by_flag(e, lambda: e.tensor_copy(counts_r[:, :, :], counts[:, :, :]).then_inc(G.sem, 1),
                                       lambda: e.memset(most[:, :], 0.0).then_inc(G.sem, 1)))
        counts_rounded = (G.sem, G.count)
        run_steps(2 * FC, LAST_STEP - 6)

        plan = Plan(W1_AT)
        w_raw = plan.take(KC, D)
        w_hi, w_lo = plan.rounded("w_hi", KC, D), plan.rounded("w_lo", KC, D)
        layer_bias = plan.take(LAYERS, D)
        trans3 = plan.take(KC, P)
        assert plan.at <= SIZE
        plan = Plan(0, W1_AT)
        hw_hi = [plan.rounded(f"hw_hi{i}", NB, D) for i in range(2)]
        hw_lo = [plan.rounded(f"hw_lo{i}", NB, D) for i in range(2)]
        plan = Plan(second_at, W1_AT)
        w_first = plan.take(KC, D)
        trans_hi = [plan.rounded(f"trans_hi{i}", KC, P) for i in range(2)]
        trans_lo = [plan.rounded(f"trans_lo{i}", KC, P) for i in range(2)]
        h = [plan.take(D) for _ in range(2)]
        rows3 = [plan.take(D) for _ in range(2)]
        in_float32r = [True]

        l_lw, l_lb, l_out = landing("layer_w"), landing("layer_bias"), landing("out")

        def load_w(i, raw, after):
            return l_lw.dma(S, lambda e: e.dma_start(raw, w_view(ins["L1_gnn_W"][i, :, :])), after)

        def split_w(raw, loaded, read):
            t = A.do(lambda e: e.activation(w_hi, raw, ACT.Copy), loaded, read)
            return V.do(lambda e: e.tensor_tensor(w_lo, raw, as_float(w_hi), ALU.subtract), t, read)
        lw = load_w(0, w_first, slot_read[1])
        rows_read, rows_done = [rest_ready[NB - 1]] * 2, [turned_b[NB - 1]] * 2
        turned_t, turn_free, trans3_free, trans_read = [None] * 2, [None] * 2, None, [None] * 2
        mul_free, agg_free = [None] * 2, [None] * 2
        hw_ready = {}

        def rows_of(b, *after):
            st = moments_of(h[b % 2], *after)
            rows_done[b % 2] = apply_moments(st, rows3[b % 2], h[b % 2], rows_read[b % 2])

        def turn_of(i, b):
            s = b % 2
            rows_read[s], t = turn(rows3[s], trans3, ("L1_gnn_ln_g", i * KC), ("L1_gnn_ln_b", i * KC), s, trans3_free, turn_free[s], rows_done[s])
            turn_free[s] = t
            turned_t[s] = A.do(lambda e: e.activation(trans_hi[s], trans3, ACT.Copy), t, trans_read[s])

        def small_of(b):
            nonlocal trans3_free
            s = b % 2
            turned_t[s] = trans3_free = V.do(lambda e: e.tensor_tensor(trans_lo[s], trans3, as_float(trans_hi[s]), ALU.subtract), turned_t[s])

        def project_of(i, b):
            s = b % 2
            terms = [(lhs, rhs, k) for lhs, rhs in three((trans_hi[s], trans_lo[s]), (w_hi, w_lo)) for k in range(KC)]
            for n, (lhs, rhs, k) in enumerate(terms):
                t = T.do(lambda e, lhs=lhs, rhs=rhs, k=k, n=n: e.matmul(bank[:, 6 + s, :], lhs[:, k, :], rhs[:, k, :], start=(n == 0), stop=(n == len(terms) - 1)),
                         turned_t[s], split_done, mul_free[s])
            trans_read[s] = t
            t = A.do(lambda e: e.activation(hw_hi[i % 2][:, b, :], bank[:, 6 + s, :], ACT.Copy, scale=norm_src[:, b:b + 1]), t, norms["ready"])
            mul_free[s] = hw_ready[i, b] = V.do(lambda e: e.scalar_tensor_tensor(hw_lo[i % 2][:, b, :], bank[:, 6 + s, :], norm_src[:, b:b + 1], as_float(hw_hi[i % 2][:, b, :]), ALU.mult, ALU.subtract), t)

        def aggregate(i, b, sources):
            n = min(P, N - b * P)
            for s in sources:
                for part in (hw_hi, hw_lo):
                    def product(e, s=s, part=part):
                        lhs, rhs = counts_r[:, s, b * P:b * P + n], part[i % 2][:, s, :]
                        if not in_float32r[0]:
                            lhs, rhs = counts[:, s, b * P:b * P + n], as_float(rhs)
                        return e.matmul(bank[0:n, 4 + b % 2, :], lhs, rhs, start=(s == 0 and part is hw_hi), stop=(s == NB - 1 and part is hw_lo))
                    t = T.do(product,
                             hw_ready[i, s], counts_rounded, agg_free[b % 2])
            return t

        def finish(i, b, t):
            n = min(P, N - b * P)
            s = b % 2
            agg_free[s] = t = V.do(lambda e: e.scalar_tensor_tensor(h[s][0:n, :], bank[0:n, 4 + s, :], norm_dst[0:n, b:b + 1], layer_bias[0:n, i, :], ALU.mult, ALU.add), t, rows_done[s], bias_loaded)
            if i < LAYERS - 1:
                t = V.do(lambda e: e.tensor_scalar(h[s][0:n, :], h[s][0:n, :], 0.0, None, ALU.max), t)
                rows_of(b, t)
            else:
                t = V.do(lambda e: e.tensor_tensor(state[0:n, b, :], h[s][0:n, :], state[0:n, b, :], ALU.add), t)
                rows_done[s] = t
                l_out.dma(S, lambda e: e.dma_start(out[b * P:b * P + n, :], state[0:n, b, :]), t)

        def by_flag(e, exact, otherwise):
            e.cond(e.value_load(exact_flag[0:1, 0:1], min_val=0, max_val=1), exact, otherwise)

        first_h = [None] * NB

        def relu_norm(b):
            first_h[b] = A.do(lambda e: e.activation(h[b % 2], state[:, b, :], ACT.Relu, bias=x2_shift[:, b:b + 1], scale=x2_scale[:, b:b + 1]), x2_ready[b], rows_done[b % 2], rest_ready[NB - 1])

        relu_norm(0)
        relu_norm(1)
        st = [moments_of(h[b], first_h[b]) for b in range(2)]
        for b in range(2):
            rows_done[b] = apply_moments(st[b], rows3[b], h[b], rows_read[b])
        run_steps(LAST_STEP - 6, LAST_STEP)
        activate(LAST_STEP)
        w1_read = hidden_at[LAST_STEP]
        for i in range(LAYERS):
            bias_loaded = l_lb.dma(S, lambda e, i=i: e.dma_start(layer_bias[:, i, :], spread(ins["L1_gnn_b"][i, :])), w1_read)
        split_done = split_w(w_first, lw, w1_read)
        turn_free = [hid_free[0], hid_free[1]]
        trans3_free = w1_read
        turn_of(0, 0)
        small_of(0)
        relu_norm(2)
        output_product(LAST_STEP)
        add_output(steps[LAST_STEP][0])
        for _ in moments_behind(steps[LAST_STEP][0]):
            pass
        for b in range(1, NB):
            turn_of(0, b)
            if b + 1 < NB:
                st = moments_of(h[(b + 1) % 2], first_h[b + 1])
            small_of(b)
            if b + 1 < NB:
                rows_done[(b + 1) % 2] = apply_moments(st, rows3[(b + 1) % 2], h[(b + 1) % 2], rows_read[(b + 1) % 2])
            if b + 2 < NB:
                relu_norm(b + 2)
            project_of(0, b - 1)
        T.wait(norms["flag"])
        before = len(T.ops)
        for i in range(LAYERS):
            sums = {}
            aggregate(i, 0, range(NB - 4))
            if i:
                turn_of(i, NB - 1)
                small_of(NB - 1)
            aggregate(i, 1, range(NB - 4))
            if i:
                project_of(i, NB - 2)
            project_of(i, NB - 1)
            for b in range(2):
                aggregate(i, b, range(NB - 4, NB - 1))
            for b in range(2):
                sums[b] = aggregate(i, b, [NB - 1])
            for b in range(NB):
                if b not in sums:
                    sums[b] = aggregate(i, b, range(NB))
                if i < LAYERS - 1 and b == 2:
                    turn_of(i + 1, 0)
                    small_of(0)
                finish(i, b, sums[b])
                if i == LAYERS - 1:
                    continue
                if b == 1:
                    split_done = split_w(w_raw, load_w(i + 1, w_raw, split_done), trans_read[(NB - 1) % 2])
                if b >= 2:
                    turn_of(i + 1, b - 1)
                    small_of(b - 1)
                    project_of(i + 1, b - 2)

        convolutions = T.ops[before:]
        del T.ops[before:]

        def lay_down(e, exact):
            in_float32r[0] = exact
            for op in convolutions:
                op(e)
        T.ops.append(lambda e: by_flag(e, lambda: lay_down(e, True), lambda: lay_down(e, False)))

        for l in landings:
            S.wait((l.sem, l.count))
        with nc.Block() as block:
            block.vector(V.run)
            block.scalar(A.run)
            block.tensor(T.run)
            block.gpsimd(G.run)
            block.sync(S.run)


_INS = ['x', 'src', 'dst', 'L0_gnn_ln1_g', 'L0_gnn_ln1_b', 'L0_gnn_Wl', 'L0_gnn_Wr', 'L0_gnn_att', 'L0_gnn_gat_bias',
        'L0_gnn_ln2_g', 'L0_gnn_ln2_b', 'L0_gnn_W1', 'L0_gnn_b1', 'L0_gnn_W2', 'L0_gnn_b2', 'L1_gnn_ln_g', 'L1_gnn_ln_b',
        'L1_gnn_W', 'L1_gnn_b']


def kernel(**inputs):
    import numpy as _np
    import concourse.bacc as _bacc
    from concourse import mybir as _mybir
    from concourse.bass_utils import run_bass_kernel_spmd as _run

    nc = _bacc.Bacc("TRN2", target_bir_lowering=False, num_devices=1)
    arrays, args = {}, {}
    for name in _INS:
        a = _np.ascontiguousarray(inputs[name])
        arrays[f"in_{name}_dram"] = a
        args[name] = nc.dram_tensor(f"in_{name}_dram", a.shape, _mybir.dt.from_np(a.dtype), kind="ExternalInput").ap()
    out = nc.dram_tensor("out_0_dram", args["x"].shape, _mybir.dt.float32, kind="ExternalOutput").ap()
    build(nc, args, out)
    r = _run(nc, [arrays], core_ids=[0])
    return r.results[0]["out_0_dram"]
```
